# Optimizing a Trainium2 kernel written in Bass

```python
import numpy as np
import jax
import jax.numpy as jnp

def _softmax(x, axis=-1):
    return jax.nn.softmax(x, axis=axis)

def _gelu(x):
    return jax.nn.gelu(x, approximate=True)

def _silu(x):
    return jax.nn.silu(x)

def _sigmoid(x):
    return jax.nn.sigmoid(x)

def _layernorm(x, axis=-1, eps=1e-05):
    m = jnp.mean(x, axis=axis, keepdims=True)
    v = jnp.var(x, axis=axis, keepdims=True)
    return (x - m) / jnp.sqrt(v + eps)

def _scatter_add(tgt, idx, src, axis=0):
    return tgt.at[idx].add(src)

def _segment_sum(src, seg, n):
    return jax.ops.segment_sum(src, seg, n)
kernel_name = 'mk_gnn_preln_d4_gnn_r16_44d90b'

def setup_inputs(seed: int=0):
    np.random.seed(seed)
    _w = jnp.asarray

    def _rec_inputs():
        import jax
        import jax.numpy as jnp
        _gk = jax.random.key(seed)
        x = -0.000202 + 1 * jax.random.normal(jax.random.fold_in(_gk, 1), (3125, 128), jnp.float32)
        src = jax.random.randint(jax.random.fold_in(_gk, 2), (100000,), 0, 3125, jnp.int32)
        dst = jax.random.randint(jax.random.fold_in(_gk, 3), (100000,), 0, 3125, jnp.int32)
        _o = jnp.argsort(dst, stable=True)
        src = src[_o]
        dst = dst[_o]
        edge_type_8 = jax.random.randint(jax.random.fold_in(_gk, 14), (100000,), 0, 8, jnp.int32)
        return (x, src, dst, edge_type_8)
    x, src, dst, edge_type_8 = _rec_inputs()

    def _L0_gnn_setup():
        import jax, jax.numpy as jnp
        import numpy as np
        N_NODES = 3125
        N_EDGES = 50000
        IN_FEAT = 128
        OUT_FEAT = 128
        NUM_RELS = 8
        key = jax.random.key(seed)
        k_h, k_w, k_b, k_s, k_d, k_r = jax.random.split(key, 6)
        return {'h': jax.random.normal(k_h, (N_NODES, IN_FEAT), dtype=jnp.float32), 'weight': jax.random.normal(k_w, (NUM_RELS + 1, IN_FEAT, OUT_FEAT), dtype=jnp.float32) * (1.0 / np.sqrt(IN_FEAT)), 'bias': jax.random.normal(k_b, (NUM_RELS + 1, OUT_FEAT), dtype=jnp.float32) * 0.02, 'src': jax.random.randint(k_s, (N_EDGES,), 0, N_NODES, dtype=jnp.int32), 'dst': jax.random.randint(k_d, (N_EDGES,), 0, N_NODES, dtype=jnp.int32), 'rel': jax.random.randint(k_r, (N_EDGES,), 0, NUM_RELS, dtype=jnp.int32)}
    _L0_gnn_all = _L0_gnn_setup()
    _L0_gnn_in = {k: v for k, v in _L0_gnn_all.items() if k in ('weight', 'bias')}
    del _L0_gnn_all

    def _L1_gnn_setup():
        import jax, jax.numpy as jnp
        import numpy as np
        N_NODES = 6250
        N_EDGES = 100000
        D_FEAT = 128
        HIDDEN = 128
        BN_EPS = 0.001
        key = jax.random.key(seed)
        ks = jax.random.split(key, 8)
        h = jax.random.normal(ks[0], (N_NODES, D_FEAT), dtype=jnp.float32)
        edge_index = jax.random.randint(ks[1], (N_EDGES, 2), 0, N_NODES, dtype=jnp.int64)
        W1 = jax.random.normal(ks[2], (D_FEAT, HIDDEN), dtype=jnp.float32) * (1.0 / np.sqrt(D_FEAT))
        b1 = jnp.zeros((HIDDEN,), dtype=jnp.float32)
        gamma = jnp.ones((HIDDEN,), dtype=jnp.float32)
        beta = jnp.zeros((HIDDEN,), dtype=jnp.float32)
        mov_mean = jax.random.normal(ks[3], (HIDDEN,), dtype=jnp.float32) * 0.1
        mov_var = jax.random.uniform(ks[4], (HIDDEN,), dtype=jnp.float32, minval=0.5, maxval=1.5)
        W2 = jax.random.normal(ks[5], (HIDDEN, HIDDEN), dtype=jnp.float32) * (1.0 / np.sqrt(HIDDEN))
        b2 = jnp.zeros((HIDDEN,), dtype=jnp.float32)
        return {'h': h, 'edge_index': edge_index, 'num_nodes': N_NODES, 'W1': W1, 'b1': b1, 'gamma': gamma, 'beta': beta, 'mov_mean': mov_mean, 'mov_var': mov_var, 'W2': W2, 'b2': b2}
    _L1_gnn_all = _L1_gnn_setup()
    _L1_gnn_in = {k: v for k, v in _L1_gnn_all.items() if k in ('W1', 'b1', 'gamma', 'beta', 'mov_mean', 'mov_var', 'W2', 'b2')}
    del _L1_gnn_all

    def _L2_gnn_setup():
        import jax, jax.numpy as jnp
        import numpy as np
        N = 6250
        E = 100000
        R = 8
        D = 128

        def _rel_conv(h, W, loop_w, b, src, dst, etype, relu):
            h_rel = jnp.einsum('ni,rio->rno', h, W)
            msg = h_rel[etype, src]
            agg = jax.ops.segment_sum(msg, dst, num_segments=h.shape[0])
            out = agg + h @ loop_w + b
            return jax.nn.relu(out) if relu else out
        key = jax.random.key(seed)
        ks = jax.random.split(key, 10)
        feats = jax.random.normal(ks[0], (N, D), dtype=jnp.float32)
        src = jax.random.randint(ks[1], (E,), 0, N, dtype=jnp.int32)
        dst = jax.random.randint(ks[2], (E,), 0, N, dtype=jnp.int32)
        etype = jax.random.randint(ks[3], (E,), 0, R, dtype=jnp.int32)
        s = 0.05
        W1 = jax.random.normal(ks[4], (R, D, D), dtype=jnp.float32) * s
        loop_w1 = jax.random.normal(ks[5], (D, D), dtype=jnp.float32) * s
        b1 = jnp.zeros((D,), dtype=jnp.float32)
        W2 = jax.random.normal(ks[6], (R, D, D), dtype=jnp.float32) * s
        loop_w2 = jax.random.normal(ks[7], (D, D), dtype=jnp.float32) * s
        b2 = jnp.zeros((D,), dtype=jnp.float32)
        return {'feats': feats, 'W1': W1, 'loop_w1': loop_w1, 'b1': b1, 'W2': W2, 'loop_w2': loop_w2, 'b2': b2, 'src': src, 'dst': dst, 'etype': etype}
    _L2_gnn_all = _L2_gnn_setup()
    _L2_gnn_in = {k: v for k, v in _L2_gnn_all.items() if k in ('W1', 'loop_w1', 'b1', 'W2', 'loop_w2', 'b2')}
    del _L2_gnn_all

    def _L3_gnn_setup():
        import jax, jax.numpy as jnp
        import numpy as np
        N_NODES = 3125
        N_EDGES = 37500
        D_IN = 128
        D_HID = 128
        N_LAYERS = 4
        LN_EPS = 1e-05
        key = jax.random.key(seed)
        ks = jax.random.split(key, 8)
        x = jax.random.normal(ks[0], (N_NODES, D_IN), dtype=jnp.float32)
        edge_index = jax.random.randint(ks[1], (2, N_EDGES), 0, N_NODES, dtype=jnp.int64)
        s_in = 1.0 / np.sqrt(D_IN)
        s_h = 1.0 / np.sqrt(D_HID)
        W_in = jax.random.uniform(ks[2], (D_IN, D_HID), jnp.float32, -s_in, s_in)
        b_in = jax.random.uniform(ks[3], (D_HID,), jnp.float32, -s_in, s_in)
        Wc = jax.random.uniform(ks[4], (N_LAYERS, D_HID, D_HID), jnp.float32, -s_h, s_h)
        bc = jax.random.uniform(ks[5], (N_LAYERS, D_HID), jnp.float32, -s_h, s_h)
        ln_g = jnp.ones((N_LAYERS, D_HID), jnp.float32)
        ln_b = jnp.zeros((N_LAYERS, D_HID), jnp.float32)
        return {'x': x, 'edge_index': edge_index, 'W_in': W_in, 'b_in': b_in, 'Wc': Wc, 'bc': bc, 'ln_g': ln_g, 'ln_b': ln_b}
    _L3_gnn_all = _L3_gnn_setup()
    _L3_gnn_in = {k: v for k, v in _L3_gnn_all.items() if k in ('W_in', 'b_in', 'Wc', 'bc', 'ln_g', 'ln_b')}
    del _L3_gnn_all
    return {'x': x, 'src': src, 'dst': dst, 'edge_type_8': edge_type_8, 'L0_gnn_weight': _L0_gnn_in['weight'], 'L0_gnn_bias': _L0_gnn_in['bias'], 'L1_gnn_W1': _L1_gnn_in['W1'], 'L1_gnn_b1': _L1_gnn_in['b1'], 'L1_gnn_gamma': _L1_gnn_in['gamma'], 'L1_gnn_beta': _L1_gnn_in['beta'], 'L1_gnn_mov_mean': _L1_gnn_in['mov_mean'], 'L1_gnn_mov_var': _L1_gnn_in['mov_var'], 'L1_gnn_W2': _L1_gnn_in['W2'], 'L1_gnn_b2': _L1_gnn_in['b2'], 'L2_gnn_W1': _L2_gnn_in['W1'], 'L2_gnn_loop_w1': _L2_gnn_in['loop_w1'], 'L2_gnn_b1': _L2_gnn_in['b1'], 'L2_gnn_W2': _L2_gnn_in['W2'], 'L2_gnn_loop_w2': _L2_gnn_in['loop_w2'], 'L2_gnn_b2': _L2_gnn_in['b2'], 'L3_gnn_W_in': _L3_gnn_in['W_in'], 'L3_gnn_b_in': _L3_gnn_in['b_in'], 'L3_gnn_Wc': _L3_gnn_in['Wc'], 'L3_gnn_bc': _L3_gnn_in['bc'], 'L3_gnn_ln_g': _L3_gnn_in['ln_g'], 'L3_gnn_ln_b': _L3_gnn_in['ln_b']}

def reference(x, src, dst, edge_type_8, L0_gnn_weight, L0_gnn_bias, L1_gnn_W1, L1_gnn_b1, L1_gnn_gamma, L1_gnn_beta, L1_gnn_mov_mean, L1_gnn_mov_var, L1_gnn_W2, L1_gnn_b2, L2_gnn_W1, L2_gnn_loop_w1, L2_gnn_b1, L2_gnn_W2, L2_gnn_loop_w2, L2_gnn_b2, L3_gnn_W_in, L3_gnn_b_in, L3_gnn_Wc, L3_gnn_bc, L3_gnn_ln_g, L3_gnn_ln_b):
    import jax
    import jax.numpy as jnp

    def _L0_gnn_ref(h, weight, bias, src, dst, rel):
        import jax, jax.numpy as jnp
        import numpy as np
        N_NODES = 3125
        N_EDGES = 50000
        IN_FEAT = 128
        OUT_FEAT = 128
        NUM_RELS = 8
        n = h.shape[0]
        hw = jnp.einsum('ni,rio->rno', h, weight)
        msg = hw[rel, src] + bias[rel]
        agg = jax.ops.segment_max(msg, dst, num_segments=n)
        in_deg = jax.ops.segment_sum(jnp.ones((msg.shape[0],), dtype=jnp.int32), dst, num_segments=n)
        agg = jnp.where((in_deg > 0)[:, None], agg, 0.0)
        out = hw[-1] + agg + bias[-1]
        return jax.nn.relu(out)

    def _L1_gnn_ref(h, edge_index, num_nodes, W1, b1, gamma, beta, mov_mean, mov_var, W2, b2):
        import jax, jax.numpy as jnp
        import numpy as np
        N_NODES = 6250
        N_EDGES = 100000
        D_FEAT = 128
        HIDDEN = 128
        BN_EPS = 0.001
        src = edge_index[:, 0]
        dst = edge_index[:, 1]
        messages = h[src]
        agg = jax.ops.segment_sum(messages, dst, num_segments=num_nodes)
        x = h + agg
        x = x @ W1 + b1
        inv = jax.lax.rsqrt(mov_var + BN_EPS)
        x = (x - mov_mean) * inv * gamma + beta
        x = jax.nn.relu(x)
        x = x @ W2 + b2
        return jax.nn.relu(x)

    def _L2_gnn_ref(feats, W1, loop_w1, b1, W2, loop_w2, b2, src, dst, etype):
        import jax, jax.numpy as jnp
        import numpy as np
        N = 6250
        E = 100000
        R = 8
        D = 128

        def _rel_conv(h, W, loop_w, b, src, dst, etype, relu):
            h_rel = jnp.einsum('ni,rio->rno', h, W)
            msg = h_rel[etype, src]
            agg = jax.ops.segment_sum(msg, dst, num_segments=h.shape[0])
            out = agg + h @ loop_w + b
            return jax.nn.relu(out) if relu else out
        h = _rel_conv(feats, W1, loop_w1, b1, src, dst, etype, relu=True)
        h = _rel_conv(h, W2, loop_w2, b2, src, dst, etype, relu=False)
        return h

    def _L3_gnn_ref(x, edge_index, W_in, b_in, Wc, bc, ln_g, ln_b):
        import jax, jax.numpy as jnp
        import numpy as np
        N_NODES = 3125
        N_EDGES = 37500
        D_IN = 128
        D_HID = 128
        N_LAYERS = 4
        LN_EPS = 1e-05
        N = x.shape[0]
        loops = jnp.arange(N, dtype=edge_index.dtype)
        src = jnp.concatenate([edge_index[0], loops])
        dst = jnp.concatenate([edge_index[1], loops])
        deg = jax.ops.segment_sum(jnp.ones_like(dst, dtype=x.dtype), dst, num_segments=N)
        dis = jnp.where(deg > 0, jax.lax.rsqrt(jnp.maximum(deg, 1.0)), 0.0)
        norm = dis[src] * dis[dst]
        h = x @ W_in + b_in
        for i in range(Wc.shape[0]):
            t = h @ Wc[i]
            msg = t[src] * norm[:, None]
            agg = jax.ops.segment_sum(msg, dst, num_segments=N) + bc[i]
            y = h + jax.nn.relu(agg)
            mu = jnp.mean(y, axis=-1, keepdims=True)
            var = jnp.mean(jnp.square(y - mu), axis=-1, keepdims=True)
            h = (y - mu) * jax.lax.rsqrt(var + LN_EPS) * ln_g[i] + ln_b[i]
        return h
    edge_index = jnp.stack([src, dst])
    edge_index_t = jnp.stack([src, dst], axis=1)
    h = jnp.maximum(_layernorm(x, axis=-1), 0.0)
    x = x + _L0_gnn_ref(h, L0_gnn_weight, L0_gnn_bias, src, dst, edge_type_8)
    h = jnp.maximum(_layernorm(x, axis=-1), 0.0)
    x = x + _L1_gnn_ref(h, edge_index_t, 3125, L1_gnn_W1, L1_gnn_b1, L1_gnn_gamma, L1_gnn_beta, L1_gnn_mov_mean, L1_gnn_mov_var, L1_gnn_W2, L1_gnn_b2)
    h = jnp.maximum(_layernorm(x, axis=-1), 0.0)
    x = x + _L2_gnn_ref(h, L2_gnn_W1, L2_gnn_loop_w1, L2_gnn_b1, L2_gnn_W2, L2_gnn_loop_w2, L2_gnn_b2, src, dst, edge_type_8)
    h = jnp.maximum(_layernorm(x, axis=-1), 0.0)
    x = x + _L3_gnn_ref(h, edge_index, L3_gnn_W_in, L3_gnn_b_in, L3_gnn_Wc, L3_gnn_bc, L3_gnn_ln_g, L3_gnn_ln_b)
    return x

_drawn_inputs = setup_inputs


def setup_inputs(seed=0):
    import zlib

    import numpy as np

    out = dict(_drawn_inputs(seed))
    spreads = {'L1_gnn_b1': (0.0, 0.8),
     'L1_gnn_gamma': (1.0, 0.2),
     'L1_gnn_beta': (0.0, 0.8),
     'L1_gnn_b2': (0.0, 0.766),
     'L2_gnn_b1': (0.0, 0.609),
     'L2_gnn_b2': (0.0, 2.0),
     'L3_gnn_ln_g': (1.0, 0.6),
     'L3_gnn_ln_b': (0.0, 0.8)}
    factors = {'L0_gnn_bias': 2.769,
     'L1_gnn_mov_mean': 8.0,
     'L3_gnn_b_in': 26.114,
     'L3_gnn_Wc': 3.144,
     'L3_gnn_bc': 28.474,
     'L3_gnn_W_in': 3.474}
    for name, (base, spread) in spreads.items():
        noise = np.random.default_rng([zlib.crc32(name.encode()), seed]).standard_normal(out[name].shape)
        drawn = base * np.exp(spread * noise) if base else spread * noise
        out[name] = jnp.asarray(drawn.astype(out[name].dtype))
    for name, factor in factors.items():
        out[name] = (out[name] * factor).astype(out[name].dtype)
    return out
```

```python
from contextlib import ExitStack

import numpy as np
import concourse.bass as bass
from concourse import mybir

F32, BF16, I32 = mybir.dt.float32, mybir.dt.bfloat16, mybir.dt.int32
ALU = mybir.AluOpType
ACT = mybir.ActivationFunctionType
AX = mybir.AxisListType

P = 128
N = 3125
E = 100000
D = 128
R = 8
NT = -(-N // P)
NP = NT * P
LAST = N - (NT - 1) * P
STEPS = -(-E // P)
HALF = 17
ROUNDS = STEPS // (2 * HALF)
CHUNK = 23
HROUNDS = STEPS // (2 * CHUNK)
TILES = 5
TROUNDS = NT // TILES
W9 = (R + 1) * D
BIG = 3.0e38
assert ROUNDS * 2 * HALF == STEPS and HROUNDS * 2 * CHUNK == STEPS and TROUNDS * TILES == NT


class Chain:

    def __init__(self, eng, sem):
        self.eng, self.sem, self.n = eng, sem, 0

    def __call__(self, ins):
        self.n += 1
        ins.then_inc(self.sem, 1)
        self.eng.wait_ge(self.sem, self.n)


class Program:
    def __init__(self, nc, ctx):
        self.nc, self.ctx, self.count, self.sems = nc, ctx, 0, []

    def sb(self, name, shape, dt=F32):
        return self.ctx.enter_context(self.nc.sbuf_tensor(name, shape, dt))

    def sem(self, name):
        self.count += 1
        self.sems.append(self.nc.alloc_semaphore(f"{name}_{self.count}"))
        return self.sems[-1]

    def recycle(self):
        self.nc.clear_and_free_semaphores(self.sems)
        self.nc.all_engine_barrier()
        self.sems = []

    def dram(self, name, shape, dt=F32):
        return self.nc.dram_tensor(name, shape, dt).ap()


def edge_rows(ap, first, tile):
    whole = (E - first) // STEPS
    rest = E - first - whole * STEPS
    yield tile[0:whole, :], ap[first:first + whole * STEPS].rearrange("(p t) -> p t", t=STEPS)
    yield tile[whole:whole + 1, 0:rest], ap[first + whole * STEPS:E].rearrange("(a t) -> a t", a=1)


def load_nodes_and_constants(g):
    nc = g.nc
    s_fill, s_chain, s_ld, s_io, s_st = (g.sem(n) for n in ("fill", "cchain", "xload", "iota", "neutral"))
    with nc.Block() as block:
        @block.gpsimd
        def _(e):
            e.memset(g.ident[:, :], 0.0).then_inc(s_fill, 1)
            e.memset(g.upper[:, :], 1.0).then_inc(s_fill, 1)
            e.memset(g.ones[:, :], 1.0).then_inc(s_fill, 1)
            e.memset(g.X[:, NT - 1, :], 0.0).then_inc(s_fill, 1)
            e.memset(g.run[:, 0, 0, :], 0.0).then_inc(s_fill, 1)
            e.memset(g.run[:, 0, 1, :], -BIG).then_inc(s_fill, 1)
            e.wait_ge(s_fill, 6)
            e.affine_select(out=g.ident[:, :], in_=g.ident[:, :], compare_op=ALU.not_equal, fill=1.0,
                            base=0, pattern=[[-1, P]], channel_multiplier=1).then_inc(s_io, 1)
            e.affine_select(out=g.upper[:, :], in_=g.upper[:, :], compare_op=ALU.is_ge, fill=0.0,
                            base=0, pattern=[[1, P]], channel_multiplier=-1).then_inc(s_io, 1)
            e.iota(g.iota_i[:, 0:P], pattern=[[1, P]], base=0, channel_multiplier=0).then_inc(s_io, 1)
            e.iota(g.iota_i[:, P:2 * P], pattern=[[STEPS, P]], base=0, channel_multiplier=0).then_inc(s_io, 1)

        @block.vector
        def _(e):
            e.wait_ge(s_io, 4)
            e.tensor_copy(g.iota_b[:, :], g.iota_i[:, 0:P]).then_inc(s_chain, 1)
            e.tensor_copy(g.block0[:, :], g.iota_i[:, P:2 * P]).then_inc(s_chain, 1)

        @block.sync
        def _(e):
            with e.Fori(0, NT - 1) as j:
                e.dma_start(g.X[:, bass.ds(j, 1), :].rearrange("p a f -> p (a f)"),
                            g.x[bass.ds(j * P, P), :]).then_inc(s_ld, 16)
            e.wait_ge(s_fill, 6)
            e.dma_start(g.X[0:LAST, NT - 1, :], g.x[N - LAST:N, :]).then_inc(s_ld, 16)
            e.dma_start(g.running[P * STEPS:P * STEPS + 1, :], g.run[0:1, 0, 0, :]).then_inc(s_st, 16)
            e.dma_start(g.carry_sum[0:1, :], g.run[0:1, 0, 0, :]).then_inc(s_st, 16)
            e.dma_start(g.carry_max[0:1, :], g.run[0:1, 0, 1, :]).then_inc(s_st, 16)
            e.wait_ge(s_ld, 16 * NT)
            e.wait_ge(s_st, 48)


def prepare_edges(g):
    nc = g.nc
    s_fill, s_ld, s_chain, s_oh, s_mm, s_ps = (g.sem(n) for n in ("efill", "eload", "echain", "onehot", "hist", "prefix"))
    s_d = g.sem("hlast")
    hist, totals = g.ps_out[:, 0, 0:NT], g.ps_out[:, 1, 0:NT]
    with ExitStack() as tmp:
        def sb(name, shape, dt=F32):
            return tmp.enter_context(nc.sbuf_tensor(name, shape, dt))
        dst, before, rel = (sb(n, [P, STEPS], I32) for n in ("dst_i", "before_i", "rel_i"))
        low_i = sb("low_i", [P, STEPS], I32)
        low, high, relf = (sb(n, [P, STEPS]) for n in ("low", "high", "relf"))
        oh_low = sb("oh_low", [P, 2, CHUNK, P], BF16)
        oh_high = sb("oh_high", [P, 2, CHUNK, NT], BF16)
        zero = sb("zero_b", [P, P], BF16)
        incl, tot, base, start, last, blk, first = (sb(n, [P, NT]) for n in (
            "incl", "tot", "base", "start", "last", "blk", "first"))
        cmp = sb("cmp", [P, NT, P])
        diag = sb("diag", [P, P])
        g_all = sb("g_all", [P, 1])
        with nc.Block() as block:
            @block.gpsimd
            def _(e):
                e.memset(dst[:, :], NP - 1).then_inc(s_fill, 1)
                e.memset(before[:, :], NP - 1).then_inc(s_fill, 1)
                e.memset(g.key_src[:, :], 0).then_inc(s_fill, 1)
                e.memset(rel[:, :], 0).then_inc(s_fill, 1)

            @block.sync
            def _(e):
                e.wait_ge(s_fill, 4)
                for ap, tile in ((g.dst, dst), (g.src, g.key_src), (g.rel, rel)):
                    for out, part in edge_rows(ap, 0, tile):
                        e.dma_start(out, part).then_inc(s_ld, 16)
                e.dma_start(before[0:1, 1:STEPS], g.dst[0:STEPS - 1].rearrange("(a t) -> a t", a=1)).then_inc(s_ld, 16)
                for out, part in edge_rows(g.dst, STEPS - 1, before[1:P, :]):
                    e.dma_start(out, part).then_inc(s_ld, 16)

            @block.vector
            def _(e):
                step = Chain(e, s_chain)
                e.memset(zero[:, :], 0.0).then_inc(s_d, 1)
                e.wait_ge(s_ld, 16 * 9)
                step(e.tensor_tensor(g.keep_sum[:, :], dst[:, :], before[:, :], ALU.is_equal))
                step(e.tensor_reduce(g_all[:, :], g.keep_sum[:, :], AX.X, ALU.min))
                step(e.memset(g.keep_sum[:, 0:1], 0.0))
                step(e.tensor_scalar(g.keep_max[:, :], g.keep_sum[:, :], BIG, -BIG, ALU.mult, ALU.add))
                step(e.tensor_scalar(relf[:, :], g.key_src[:, :], float(R), None, ALU.mult))
                step(e.tensor_tensor(g.key_rel[:, :], relf[:, :], rel[:, :], ALU.add))
                step(e.tensor_scalar(low_i[:, :], dst[:, :], P - 1, None, ALU.bitwise_and))
                step(e.tensor_copy(low[:, :], low_i[:, :]))
                step(e.tensor_tensor(high[:, :], dst[:, :], low[:, :], ALU.subtract))
                step(e.tensor_scalar(high[:, :], high[:, :], 1.0 / P, None, ALU.mult))
                step(e.tensor_scalar(diag[:, :], g.ident[:, :], g_all[:, 0:1], None, ALU.mult))
                with e.Fori(0, HROUNDS) as i:
                    for h in range(2):
                        e.wait_ge(s_mm, i * (2 * CHUNK) + (h + 1) * CHUNK)
                        at = bass.ds(i * (2 * CHUNK) + h * CHUNK, CHUNK)
                        e.tensor_tensor(oh_low[:, h], g.iota_b[:, :].unsqueeze(1).to_broadcast([P, CHUNK, P]),
                                        low[:, at].unsqueeze(2).to_broadcast([P, CHUNK, P]),
                                        ALU.is_equal).then_inc(s_oh, 1)
                        e.tensor_tensor(oh_high[:, h], g.iota_b[:, 0:NT].unsqueeze(1).to_broadcast([P, CHUNK, NT]),
                                        high[:, at].unsqueeze(2).to_broadcast([P, CHUNK, NT]),
                                        ALU.is_equal).then_inc(s_oh, 1)
                e.wait_ge(s_ps, 1)
                step(e.tensor_copy(g.degree[:, :], hist))
                e.wait_ge(s_ps, 2)
                step(e.tensor_copy(incl[:, :], g.ps_out[:, 0, 64:64 + NT]))
                step(e.tensor_copy(tot[:, :], totals))
                step(e.tensor_copy(g.chain_sum[:, :], g.ps_out[:, 1, 512:512 + P]))
                step(e.tensor_scalar(g.chain_max[:, :], g.chain_sum[:, :], BIG, -BIG, ALU.mult, ALU.add))
                step(e.tensor_tensor_scan(base[:, :], g.ones[:, 0:NT], tot[:, :], 0.0, ALU.mult, ALU.add))
                step(e.tensor_tensor(base[:, :], base[:, :], tot[:, :], ALU.subtract))
                step(e.tensor_tensor(incl[:, :], incl[:, :], base[:, :], ALU.add))
                step(e.tensor_tensor(start[:, :], incl[:, :], g.degree[:, :], ALU.subtract))
                step(e.tensor_scalar(last[:, :], incl[:, :], -1.0, None, ALU.add))
                step(e.tensor_tensor(cmp[:, :, :], last[:, :].unsqueeze(2).to_broadcast([P, NT, P]),
                                     g.block0[:, :].unsqueeze(1).to_broadcast([P, NT, P]), ALU.is_ge))
                step(e.tensor_reduce(blk[:, :], cmp[:, :, :], AX.X, ALU.add))
                step(e.tensor_scalar(blk[:, :], blk[:, :], -1.0, None, ALU.add))
                step(e.tensor_scalar(first[:, :], blk[:, :], float(STEPS), None, ALU.mult))
                step(e.tensor_tensor(first[:, :], start[:, :], first[:, :], ALU.is_lt))
                step(e.tensor_tensor(blk[:, :], blk[:, :], first[:, :], ALU.mult))
                step(e.tensor_scalar(tot[:, :], g.degree[:, :], 0.0, None, ALU.is_gt))
                step(e.tensor_tensor(g.carry_at[:, :], blk[:, :], tot[:, :], ALU.mult))
                step(e.tensor_scalar(last[:, :], last[:, :], float(-P * STEPS), None, ALU.add))
                step(e.tensor_tensor(last[:, :], last[:, :], tot[:, :], ALU.mult))
                step(e.tensor_scalar(g.last_at[:, :], last[:, :], float(P * STEPS), None, ALU.add))

            @block.tensor
            def _(e):
                e.sem_inc(s_mm, 2 * CHUNK)
                e.wait_ge(s_d, 1)
                e.matmul(hist, zero[:, :], zero[:, 0:NT], start=True, stop=False)
                with e.Fori(0, HROUNDS) as i:
                    for h in range(2):
                        e.wait_ge(s_oh, i * 4 + 2 * h + 2)
                        for c in range(CHUNK):
                            e.matmul(hist, oh_low[:, h, c, :], oh_high[:, h, c, :],
                                     start=False, stop=False).then_inc(s_mm, 1)
                e.matmul(hist, zero[:, :], zero[:, 0:NT], start=False, stop=True).then_inc(s_ps, 1)
                e.wait_ge(s_chain, 12)
                e.matmul(g.ps_out[:, 0, 64:64 + NT], g.upper[:, :], g.degree[:, :], start=True, stop=True)
                e.matmul(g.ps_out[:, 1, 512:512 + P], g.ones[:, :], diag[:, :], start=True, stop=True)
                e.matmul(totals, g.ones[:, :], g.degree[:, :], start=True, stop=True).then_inc(s_ps, 1)


def layer_norm(g, gain=None, shift=None, relu=True):
    nc = g.nc
    s_chain, s_v, s_r = (g.sem(n) for n in ("nchain", "var", "dev"))
    src = g.X if gain is None else g.Y
    wide = [P, NT, D]
    with nc.Block() as block:
        @block.vector
        def _(e):
            step = Chain(e, s_chain)
            step(e.tensor_reduce(g.mean[:, :], src[:, :, :], AX.X, ALU.add))
            step(e.tensor_scalar(g.mean[:, :], g.mean[:, :], -1.0 / D, None, ALU.mult))
            step(e.tensor_tensor(g.H[:, :, :], src[:, :, :], g.mean[:, :].unsqueeze(2).to_broadcast(wide), ALU.add))
            step(e.tensor_tensor(g.Z[:, :, :], g.H[:, :, :], g.H[:, :, :], ALU.mult))
            step(e.tensor_reduce(g.var[:, :], g.Z[:, :, :], AX.X, ALU.add))
            e.tensor_scalar(g.var[:, :], g.var[:, :], 1.0 / D, 1e-5, ALU.mult, ALU.add).then_inc(s_v, 1)
            e.wait_ge(s_r, 1)
            step(e.reciprocal(g.mean[:, :], g.dev[:, :]))
            step(e.tensor_tensor(g.H[:, :, :], g.H[:, :, :], g.mean[:, :].unsqueeze(2).to_broadcast(wide), ALU.mult))
            if gain is not None:
                step(e.tensor_tensor(g.H[:, :, :], g.H[:, :, :], gain.unsqueeze(1).to_broadcast(wide), ALU.mult))
                step(e.tensor_tensor(g.H[:, :, :], g.H[:, :, :], shift.unsqueeze(1).to_broadcast(wide), ALU.add))
            if relu:
                step(e.tensor_scalar(g.H[:, :, :], g.H[:, :, :], 0.0, None, ALU.max))

        @block.scalar
        def _(e):
            e.wait_ge(s_v, 1)
            e.activation(g.dev[:, :], g.var[:, :], ACT.Sqrt).then_inc(s_r, 1)


def back(k):
    return 1 if k == 0 else 2


def project(g, src, weights, cols, evacuate, hidden=None, store=None):
    nc = g.nc
    s_in, s_T, s_hT, s_mm, s_ev, s_h1, s_h2 = (g.sem(n) for n in (
        "pin", "ptrans", "pcopy", "pprod", "pevac", "phid", "prelu"))
    s_st = [g.sem(f"pstore{i}") for i in range(2)]
    stages = [(c, min(c + 512, cols)) for c in range(0, cols, 512)]

    def body(e, f):
        with e.Fori(0, TROUNDS) as i:
            for k in range(TILES):
                f(i * TILES + k, k, k % 2)

    with nc.Block() as block:
        @block.scalar
        def _(e):
            def tile(n, k, s):
                e.wait_ge(s_T, n - back(k) + 3)
                e.activation(g.tin[:, s, :], src[:, bass.ds(n, 1), :].rearrange("p a f -> p (a f)"),
                             ACT.Copy).then_inc(s_in, 1)
                e.wait_ge(s_T, n + 3)
                e.wait_ge(s_mm, n - back(k) + 3)
                e.activation(g.tT[:, s, :], g.ps_t[:, s, 0:P], ACT.Copy).then_inc(s_hT, 1)
                if hidden:
                    e.wait_ge(s_h1, n + 1)
                    e.activation(g.tH[:, s, :], g.ps_t[:, s, P:2 * P], ACT.Relu, bias=hidden[1],
                                 scale=hidden[0]).then_inc(s_h2, 1)
            body(e, tile)

        @block.tensor
        def _(e):
            e.sem_inc(s_T, 2)
            e.sem_inc(s_mm, 2)

            def tile(n, k, s):
                e.wait_ge(s_in, n + 1)
                e.wait_ge(s_hT, n - back(k) + 3)
                e.transpose(g.ps_t[:, s, 0:P], g.tin[:, s, :], g.ident[:, :]).then_inc(s_T, 1)
                e.wait_ge(s_hT, n + 3)
                if hidden:
                    e.matmul(g.ps_t[:, s, P:2 * P], weights, g.tT[:, s, :], start=True, stop=True).then_inc(s_h1, 1)
                    e.wait_ge(s_h2, n + 1)
                rows, w = (g.tH, hidden[2]) if hidden else (g.tT, weights)
                e.wait_ge(s_ev, n - back(k) + 3)
                for a, b in stages:
                    last = e.matmul(g.ps_out[:, s, a:b], rows[:, s, :], w[:, a:b], start=True, stop=True)
                last.then_inc(s_mm, 1)
            body(e, tile)

        @block.vector
        def _(e):
            e.sem_inc(s_hT, 2)
            e.sem_inc(s_ev, 2)

            def tile(n, k, s):
                e.wait_ge(s_mm, n + 3)
                if store:
                    per, done = (3, (k + 1) // 2) if s == 0 else (2, k // 2)
                    e.wait_ge(s_st[s], (i_of(n, k) * per + done) * 16 + 16)
                evacuate(e, n, s).then_inc(s_ev, 1)

            def i_of(n, k):
                return rounds[0]
            rounds = [None]
            with e.Fori(0, TROUNDS) as i:
                rounds[0] = i
                for k in range(TILES):
                    tile(i * TILES + k, k, k % 2)

        if store:
            @block.sync
            def _(e):
                for s in range(2):
                    e.dma_start(g.credit[s:s + 1, :], g.ident[0:1, 0:1]).then_inc(s_st[s], 16)

                def tile(n, k, s):
                    e.wait_ge(s_ev, n + 3)
                    store(e, n, s).then_inc(s_st[s], 16)
                body(e, tile)
                e.wait_ge(s_st[0], 16 * (3 * TROUNDS + 1))
                e.wait_ge(s_st[1], 16 * (2 * TROUNDS + 1))


def aggregate(g, table, key, op):
    nc = g.nc
    adds = op == ALU.add
    keep, chain, carry = (g.keep_sum, g.chain_sum, g.carry_sum) if adds else (g.keep_max, g.chain_max, g.carry_max)
    join = ALU.mult if adds else ALU.add
    s_idx = [g.sem(f"idx{h}") for h in range(2)]
    s_msg = [g.sem(f"msg{h}") for h in range(2)]
    s_out = [g.sem(f"rout{h}") for h in range(2)]
    s_run, s_go = g.sem("run"), g.sem("go")
    ahead = 2 * HALF + 1
    running = g.running[0:P * STEPS, :].rearrange("(p t) f -> p t f", t=STEPS)
    with nc.Block() as block:
        @block.scalar
        def _(e):
            with e.Fori(0, ROUNDS) as i:
                for h in range(2):
                    e.wait_ge(s_run, i * (2 * HALF) + (h + 1) * HALF + 1)
                    e.activation(g.idx[:, h, :], key[:, bass.ds(i * (2 * HALF) + h * HALF, HALF)],
                                 ACT.Copy).then_inc(s_idx[h], 1)

        @block.gpsimd
        def _(e):
            with e.Fori(0, ROUNDS) as i:
                for h in range(2):
                    e.wait_ge(s_idx[h], i + 1)
                    e.sem_inc(s_go, 1)
                    for k in range(HALF):
                        e.indirect_dma_start(g.msg[:, h, k, :], None, table,
                                             bass.IndirectOffsetOnAxis(g.idx[:, h, k:k + 1], 0)).then_inc(s_msg[h], 16)

        @block.vector
        def _(e):
            e.memset(g.run[:, 1, HALF - 1, :], 0.0 if adds else -BIG).then_inc(s_run, 1)
            e.sem_inc(s_run, 2 * HALF)
            with e.Fori(0, ROUNDS) as i:
                for h in range(2):
                    e.wait_ge(s_msg[h], i * (16 * HALF) + 16 * HALF)
                    e.wait_ge(s_out[h], i * 16 + 16)
                    for k in range(HALF):
                        prev = g.run[:, h, k - 1, :] if k else g.run[:, 1 - h, HALF - 1, :]
                        t = i * (2 * HALF) + (h * HALF + k)
                        e.wait_ge(s_run, t + ahead)
                        e.scalar_tensor_tensor(g.run[:, h, k, :], prev, keep[:, bass.ds(t, 1)], g.msg[:, h, k, :],
                                               join, op).then_inc(s_run, 1)

        @block.sync
        def _(e):
            for h in range(2):
                e.dma_start(g.credit[h:h + 1, :], g.ident[0:1, 0:1]).then_inc(s_out[h], 16)
            with e.Fori(0, ROUNDS) as i:
                for h in range(2):
                    e.wait_ge(s_run, i * (2 * HALF) + (h + 1) * HALF + ahead)
                    e.dma_start(running[:, bass.ds(i * (2 * HALF) + h * HALF, HALF), :],
                                g.run[:, h, :, :]).then_inc(s_out[h], 16)
            for h in range(2):
                e.wait_ge(s_out[h], 16 * (ROUNDS + 1))

    s_t, s_s, s_c, s_d, s_a = (g.sem(n) for n in ("ctrans", "cscan", "ccopy", "cstore", "agather"))
    with nc.Block() as block:
        @block.gpsimd
        def _(e):
            for j in range(NT):
                e.indirect_dma_start(g.Z[:, j, :], None, g.running,
                                     bass.IndirectOffsetOnAxis(g.last_at[:, j:j + 1], 0)).then_inc(s_a, 16)
            e.wait_ge(s_d, 16)
            for j in range(NT):
                e.indirect_dma_start(g.C[:, j, :], None, carry,
                                     bass.IndirectOffsetOnAxis(g.carry_at[:, j:j + 1], 0)).then_inc(s_a, 16)

        @block.tensor
        def _(e):
            e.transpose(g.ps_t[:, 0, 0:P], g.run[:, 1, HALF - 1, :], g.ident[:, :]).then_inc(s_t, 1)
            e.wait_ge(s_s, 1)
            e.transpose(g.ps_t[:, 1, 0:P], g.tT[:, 0, :], g.ident[:, :]).then_inc(s_t, 1)

        @block.vector
        def _(e):
            e.wait_ge(s_t, 1)
            e.tensor_tensor_scan(g.tT[:, 0, :], chain[:, :], g.ps_t[:, 0, 0:P], 0.0 if adds else -BIG,
                                 join, op).then_inc(s_s, 1)
            e.wait_ge(s_t, 2)
            e.tensor_copy(g.tT[:, 1, :], g.ps_t[:, 1, 0:P]).then_inc(s_c, 1)
            e.wait_ge(s_a, 32 * NT)
            e.tensor_tensor(g.Z[:, :, :], g.Z[:, :, :], g.C[:, :, :], op)

        @block.sync
        def _(e):
            e.wait_ge(s_c, 1)
            e.dma_start(carry[1:P + 1, :], g.tT[:, 1, :]).then_inc(s_d, 16)
            e.wait_ge(s_d, 16)


def load_params(g, pairs):
    s_w = g.sem("params")
    with g.nc.Block() as block:
        @block.sync
        def _(e):
            for out, part in pairs:
                e.dma_start(out, part).then_inc(s_w, 16)
            e.wait_ge(s_w, 16 * len(pairs))


def row(ap):
    return ap.rearrange("(a n) -> a n", a=1).to_broadcast([P, ap.shape[0]])


def vector_stage(g, f):
    s = g.sem("vstage")
    with g.nc.Block() as block:
        @block.vector
        def _(e):
            f(e, Chain(e, s))


def relational(g, table):
    def evacuate(e, n, s):
        e.tensor_tensor(g.stage[:, s, 0:512], g.ps_out[:, s, 0:512], g.bias9[:, 0:512], ALU.add)
        e.tensor_tensor(g.S[:, bass.ds(n, 1), :].rearrange("p a f -> p (a f)"), g.ps_out[:, s, R * D:W9],
                        g.bias9[:, R * D:W9], ALU.add)
        return e.tensor_tensor(g.stage[:, s, 512:1024], g.ps_out[:, s, 512:1024], g.bias9[:, 512:1024], ALU.add)

    def store(e, n, s):
        return e.dma_start(table.rearrange("(m p r) f -> p m (r f)", p=P, r=R)[:, bass.ds(n, 1), :].rearrange(
            "p a f -> p (a f)"), g.stage[:, s, :])
    project(g, g.H, g.w9, W9, evacuate, store=store)


def store_rows(g, src):
    s = g.sem("rows")
    with g.nc.Block() as block:
        @block.sync
        def _(e):
            e.dma_start(g.table1.rearrange("(j p) f -> p j f", p=P), src[:, :, :]).then_inc(s, 16)
            e.wait_ge(s, 16)


def gnn_kernel(nc, a, out):
    with ExitStack() as ctx:
        g = Program(nc, ctx)
        g.x, g.src, g.dst, g.rel = (a[n] for n in ("x", "src", "dst", "edge_type_8"))
        g.running = g.dram("running_rows", [P * STEPS + 1, D])
        g.carry_sum = g.dram("carry_rows_sum", [P + 1, D])
        g.carry_max = g.dram("carry_rows_max", [P + 1, D])
        g.table8 = g.dram("table_rel", [NP * R, D])
        g.table1 = g.dram("table_node", [NP, D])
        g.credit = g.dram("credit", [2, 1])
        g.X, g.H, g.Y, g.Z, g.C, g.S = (g.sb(n, [P, NT, D]) for n in "XHYZCS")
        g.mean, g.var, g.dev, g.degree, g.dis = (g.sb(n, [P, NT]) for n in ("mean", "var", "dev", "degree", "dis"))
        g.carry_at, g.last_at = (g.sb(n, [P, NT], I32) for n in ("carry_at", "last_at"))
        g.ident, g.upper, g.ones, g.block0 = (g.sb(n, [P, P]) for n in ("ident", "upper", "ones", "block0"))
        g.chain_sum, g.chain_max = (g.sb(n, [P, P]) for n in ("chain_sum", "chain_max"))
        g.iota_i, g.iota_b = g.sb("iota_i", [P, 2 * P], I32), g.sb("iota_b", [P, P], BF16)
        g.key_src, g.key_rel = (g.sb(n, [P, STEPS], I32) for n in ("key_src", "key_rel"))
        g.keep_sum, g.keep_max = (g.sb(n, [P, STEPS]) for n in ("keep_sum", "keep_max"))
        g.idx = g.sb("idx", [P, 2, HALF], I32)
        g.msg, g.run = (g.sb(n, [P, 2, HALF, D]) for n in ("msg", "run"))
        g.tin, g.tT, g.tH = (g.sb(n, [P, 2, D]) for n in ("tin", "tT", "tH"))
        g.stage = g.sb("stage", [P, 2, R * D])
        g.w9, g.bias9 = g.sb("w9", [P, W9]), g.sb("bias9", [P, W9])
        g.rows = g.sb("rows", [P, 4, D])
        g.cols = g.sb("cols", [P, 8])
        g.ps_t = ctx.enter_context(nc.psum_tensor("ps_t", [P, 2, 512], F32))
        g.ps_out = ctx.enter_context(nc.psum_tensor("ps_out", [P, 2, 1536], F32))

        load_nodes_and_constants(g)
        prepare_edges(g)

        load_params(g, [(g.w9[:, :].rearrange("k (r o) -> k r o", o=D),
                         a["L0_gnn_weight"].rearrange("r k o -> k r o")),
                        (g.bias9[:, :], row(a["L0_gnn_bias"].rearrange("r o -> (r o)")))])
        layer_norm(g)
        relational(g, g.table8)
        aggregate(g, g.table8, g.key_rel, ALU.max)

        def finish0(e, step):
            step(e.tensor_tensor(g.Z[:, :, :], g.Z[:, :, :], g.S[:, :, :], ALU.add))
            step(e.scalar_tensor_tensor(g.X[:, :, :], g.Z[:, :, :], 0.0, g.X[:, :, :], ALU.max, ALU.add))
        vector_stage(g, finish0)

        g.recycle()

        load_params(g, [(g.w9[:, 0:D], a["L1_gnn_W1"]), (g.w9[:, D:2 * D], a["L1_gnn_W2"]),
                        (g.rows[:, 0, :], row(a["L1_gnn_b2"]))] +
                       [(g.cols[:, c:c + 1], a[f"L1_gnn_{n}"].rearrange("(p a) -> p a", a=1))
                        for c, n in enumerate(("b1", "gamma", "beta", "mov_mean", "mov_var"))])
        layer_norm(g)
        store_rows(g, g.H)
        aggregate(g, g.table1, g.key_src, ALU.add)
        s_v, s_r, s_n = g.sem("bnv"), g.sem("bnr"), g.sem("bnc")
        with nc.Block() as block:
            @block.vector
            def _(e):
                step = Chain(e, s_n)
                e.tensor_scalar(g.cols[:, 4:5], g.cols[:, 4:5], 0.001, None, ALU.add).then_inc(s_v, 1)
                step(e.tensor_tensor(g.Z[:, :, :], g.Z[:, :, :], g.H[:, :, :], ALU.add))
                step(e.tensor_tensor(g.cols[:, 0:1], g.cols[:, 0:1], g.cols[:, 3:4], ALU.subtract))
                e.wait_ge(s_r, 1)
                step(e.reciprocal(g.cols[:, 5:6], g.cols[:, 6:7]))
                step(e.tensor_tensor(g.cols[:, 5:6], g.cols[:, 5:6], g.cols[:, 1:2], ALU.mult))
                step(e.tensor_tensor(g.cols[:, 7:8], g.cols[:, 0:1], g.cols[:, 5:6], ALU.mult))
                step(e.tensor_tensor(g.cols[:, 7:8], g.cols[:, 7:8], g.cols[:, 2:3], ALU.add))

            @block.scalar
            def _(e):
                e.wait_ge(s_v, 1)
                e.activation(g.cols[:, 6:7], g.cols[:, 4:5], ACT.Sqrt).then_inc(s_r, 1)

        def evacuate1(e, n, s):
            return e.tensor_tensor(g.S[:, bass.ds(n, 1), :].rearrange("p a f -> p (a f)"), g.ps_out[:, s, 0:D],
                                   g.rows[:, 0, :], ALU.add)
        project(g, g.Z, g.w9[:, 0:D], D, evacuate1, hidden=(g.cols[:, 5:6], g.cols[:, 7:8], g.w9[:, D:2 * D]))

        def finish1(e, step):
            step(e.scalar_tensor_tensor(g.X[:, :, :], g.S[:, :, :], 0.0, g.X[:, :, :], ALU.max, ALU.add))
        vector_stage(g, finish1)

        g.recycle()

        for n, first in (("1", True), ("2", False)):
            load_params(g, [(g.w9[:, 0:R * D].rearrange("k (r o) -> k r o", o=D), a[f"L2_gnn_W{n}"].rearrange("r k o -> k r o")),
                            (g.w9[:, R * D:W9], a[f"L2_gnn_loop_w{n}"]),
                            (g.bias9[:, R * D:W9], row(a[f"L2_gnn_b{n}"]))])
            if first:
                layer_norm(g)

                def clear(e, step):
                    step(e.memset(g.bias9[:, 0:R * D], 0.0))
                vector_stage(g, clear)
            relational(g, g.table8)
            aggregate(g, g.table8, g.key_rel, ALU.add)

            def finish2(e, step):
                step(e.tensor_tensor(g.Z[:, :, :], g.Z[:, :, :], g.S[:, :, :], ALU.add))
                if first:
                    step(e.tensor_scalar(g.H[:, :, :], g.Z[:, :, :], 0.0, None, ALU.max))
                else:
                    step(e.tensor_tensor(g.X[:, :, :], g.Z[:, :, :], g.X[:, :, :], ALU.add))
            vector_stage(g, finish2)

        g.recycle()

        layer_norm(g)
        load_params(g, [(g.w9[:, 0:D], a["L3_gnn_W_in"]), (g.rows[:, 0, :], row(a["L3_gnn_b_in"]))])
        s_v, s_r, s_n = g.sem("gv"), g.sem("gr"), g.sem("gc")
        with nc.Block() as block:
            @block.vector
            def _(e):
                e.tensor_scalar(g.var[:, :], g.degree[:, :], 1.0, None, ALU.add).then_inc(s_v, 1)
                e.wait_ge(s_r, 1)
                e.reciprocal(g.dis[:, :], g.dev[:, :]).then_inc(s_n, 1)

            @block.scalar
            def _(e):
                e.wait_ge(s_v, 1)
                e.activation(g.dev[:, :], g.var[:, :], ACT.Sqrt).then_inc(s_r, 1)

        def evacuate_in(e, n, s):
            return e.tensor_tensor(g.S[:, bass.ds(n, 1), :].rearrange("p a f -> p (a f)"), g.ps_out[:, s, 0:D],
                                   g.rows[:, 0, :], ALU.add)
        project(g, g.H, g.w9[:, 0:D], D, evacuate_in)

        def to_h(e, step):
            step(e.tensor_copy(g.H[:, :, :], g.S[:, :, :]))
        vector_stage(g, to_h)
        for i in range(4):
            load_params(g, [(g.w9[:, 0:D], a["L3_gnn_Wc"][i]), (g.rows[:, 0, :], row(a["L3_gnn_bc"][i])),
                            (g.rows[:, 1, :], row(a["L3_gnn_ln_g"][i])), (g.rows[:, 2, :], row(a["L3_gnn_ln_b"][i]))])

            def evacuate_t(e, n, s):
                return e.tensor_scalar(g.S[:, bass.ds(n, 1), :].rearrange("p a f -> p (a f)"), g.ps_out[:, s, 0:D],
                                       g.dis[:, bass.ds(n, 1)], None, ALU.mult)
            project(g, g.H, g.w9[:, 0:D], D, evacuate_t)
            store_rows(g, g.S)
            aggregate(g, g.table1, g.key_src, ALU.add)

            def combine(e, step):
                wide = [P, NT, D]
                step(e.tensor_tensor(g.Z[:, :, :], g.Z[:, :, :], g.S[:, :, :], ALU.add))
                step(e.tensor_tensor(g.Z[:, :, :], g.Z[:, :, :], g.dis[:, :].unsqueeze(2).to_broadcast(wide), ALU.mult))
                step(e.tensor_tensor(g.Z[:, :, :], g.Z[:, :, :], g.rows[:, 0, :].unsqueeze(1).to_broadcast(wide), ALU.add))
                step(e.scalar_tensor_tensor(g.Y[:, :, :], g.Z[:, :, :], 0.0, g.H[:, :, :], ALU.max, ALU.add))
            vector_stage(g, combine)
            layer_norm(g, g.rows[:, 1, :], g.rows[:, 2, :], relu=False)
            g.recycle()

        def finish3(e, step):
            step(e.tensor_tensor(g.X[:, :, :], g.X[:, :, :], g.H[:, :, :], ALU.add))
        vector_stage(g, finish3)
        s_o = g.sem("out")
        with nc.Block() as block:
            @block.sync
            def _(e):
                e.dma_start(out[0:N - LAST, :].rearrange("(j p) f -> p j f", p=P), g.X[:, 0:NT - 1, :]).then_inc(s_o, 16)
                e.dma_start(out[N - LAST:N, :], g.X[0:LAST, NT - 1, :]).then_inc(s_o, 16)
                e.wait_ge(s_o, 32)


def kernel(**inputs):
    import concourse.bacc as bacc
    from concourse.bass_utils import run_bass_kernel_spmd

    nc = bacc.Bacc("TRN2", target_bir_lowering=False, num_devices=1)
    arrays, aps = {}, {}
    for name, value in inputs.items():
        value = np.ascontiguousarray(value)
        arrays[f"in_{name}"] = value
        aps[name] = nc.dram_tensor(f"in_{name}", value.shape, mybir.dt.from_np(value.dtype), kind="ExternalInput").ap()
    out = nc.dram_tensor("out_x", (N, D), F32, kind="ExternalOutput").ap()
    gnn_kernel(nc, aps, out)
    return run_bass_kernel_spmd(nc, [arrays], core_ids=[0]).results[0]["out_x"]
```

```python
from contextlib import ExitStack

import numpy as np
import concourse.bass as bass
from concourse import mybir

F32, F16, F8 = mybir.dt.float32, mybir.dt.float16, mybir.dt.float8e4
I32, U8 = mybir.dt.int32, mybir.dt.uint8
ALU = mybir.AluOpType
ACT = mybir.ActivationFunctionType
AX = mybir.AxisListType

P = 128
N = 3125
E = 100000
D = 128
R = 8
NT = -(-N // P)
NP = NT * P
LAST = N - (NT - 1) * P
WIN = 4
HALF = P // WIN // 2
ROUNDS = NT
STEPS = ROUNDS * 2 * HALF
ROW = 64
PER = 14 * ROW
BLOCKS = PER
WTILES = 2
GROUPS = 7
NW = P * GROUPS
KW = NT * WIN
RING = 4
FAR = 5000
EXACT = 16
TILES = 5
TROUNDS = NT // TILES
W9 = (R + 1) * D
BIG = 3.0e38
TOP = 16384.0
assert P * STEPS >= E and P * PER >= E + 2 * WTILES * P and NW * WIN >= NP and TROUNDS * TILES == NT and P == 2 * ROW


class Chain:

    def __init__(self, eng, sem):
        self.eng, self.sem, self.n = eng, sem, 0

    def __call__(self, ins):
        self.n += 1
        ins.then_inc(self.sem, 1)
        self.eng.wait_ge(self.sem, self.n)


class Program:
    def __init__(self, nc, ctx):
        self.nc, self.ctx, self.count, self.sems = nc, ctx, 0, []

    def sb(self, name, shape, dt=F32):
        return self.ctx.enter_context(self.nc.sbuf_tensor(name, shape, dt))

    def sem(self, name):
        self.count += 1
        self.sems.append(self.nc.alloc_semaphore(f"{name}_{self.count}"))
        return self.sems[-1]

    def recycle(self):
        self.nc.clear_and_free_semaphores(self.sems)
        self.nc.all_engine_barrier()
        self.sems = []

    @staticmethod
    def flat(tile, dt=F32):
        row = tile[:, :, :, :].rearrange("p a b c -> p (a b c)")
        return row if dt == F32 else row.bitcast(dt)

    def dram(self, name, shape, dt=F32):
        return self.nc.dram_tensor(name, shape, dt).ap()


def edge_rows(ap, first, tile, width):
    whole = (E - first) // width
    rest = E - first - whole * width
    yield tile[0:whole, :], ap[first:first + whole * width].rearrange("(p t) -> p t", t=width)
    if rest:
        yield tile[whole:whole + 1, 0:rest], ap[first + whole * width:E].rearrange("(a t) -> a t", a=1)


def load_nodes_and_constants(g):
    nc = g.nc
    s_fill, s_chain, s_ld, s_io, s_st = (g.sem(n) for n in ("fill", "cchain", "xload", "iota", "neutral"))
    with nc.Block() as block:
        @block.gpsimd
        def _(e):
            e.memset(g.ident[:, :], 0.0).then_inc(s_fill, 1)
            e.memset(g.ones[:, :], 1.0).then_inc(s_fill, 1)
            e.memset(g.X[:, NT - 1, :], 0.0).then_inc(s_fill, 1)
            e.memset(g.run[:, 0, 0, :], 0.0).then_inc(s_fill, 1)
            e.memset(g.run[:, 0, 1, :], -BIG).then_inc(s_fill, 1)
            for m in (g.shift, g.corner):
                e.memset(m[:, :], 0.0).then_inc(s_fill, 1)
            e.memset(g.past[:, :], E // ROW + 1).then_inc(s_fill, 1)
            e.wait_ge(s_fill, 8)
            e.affine_select(out=g.shift[:, :], in_=g.shift[:, :], compare_op=ALU.not_equal, fill=1.0,
                            base=-1, pattern=[[1, P]], channel_multiplier=-1).then_inc(s_io, 1)
            e.affine_select(out=g.corner[:, :], in_=g.corner[:, :], compare_op=ALU.not_equal, fill=1.0,
                            base=P - 1, pattern=[[1, P]], channel_multiplier=-1).then_inc(s_io, 1)
            e.affine_select(out=g.ident[:, :], in_=g.ident[:, :], compare_op=ALU.not_equal, fill=1.0,
                            base=0, pattern=[[-1, P]], channel_multiplier=1).then_inc(s_io, 1)
            e.iota(g.iota_i[:, 0:P], pattern=[[1, P]], base=0, channel_multiplier=0).then_inc(s_io, 1)
            e.iota(g.iota_i[:, P:2 * P], pattern=[[STEPS, P]], base=0, channel_multiplier=0).then_inc(s_io, 1)
            e.iota(g.iota_i[:, 2 * P:2 * P + NT], pattern=[[P, NT]], base=0, channel_multiplier=1).then_inc(s_io, 1)
            e.iota(g.iota_w[:, :], pattern=[[WIN, NW]], base=0, channel_multiplier=0).then_inc(s_io, 1)

        @block.vector
        def _(e):
            e.wait_ge(s_io, 7)
            e.tensor_copy(g.iota_h[:, :], g.iota_i[:, 0:P]).then_inc(s_chain, 1)
            e.memset(g.zero_h[:, :], 0.0).then_inc(s_chain, 1)
            e.tensor_copy(g.block0[:, :], g.iota_i[:, P:2 * P]).then_inc(s_chain, 1)
            e.tensor_copy(g.node[:, :], g.iota_i[:, 2 * P:2 * P + NT]).then_inc(s_chain, 1)
            e.tensor_copy(g.window0[:, :], g.iota_w[:, :]).then_inc(s_chain, 1)

        @block.sync
        def _(e):
            with e.Fori(0, NT - 1) as j:
                e.dma_start(g.X[:, bass.ds(j, 1), :].rearrange("p a f -> p (a f)"),
                            g.x[bass.ds(j * P, P), :]).then_inc(s_ld, 16)
            e.wait_ge(s_fill, 8)
            e.dma_start(g.X[0:LAST, NT - 1, :], g.x[N - LAST:N, :]).then_inc(s_ld, 16)
            e.dma_start(g.running[P * STEPS:P * STEPS + 1, :], g.run[0:1, 0, 0, :]).then_inc(s_st, 16)
            e.dma_start(g.carry_sum[0:1, :], g.run[0:1, 0, 0, :]).then_inc(s_st, 16)
            e.dma_start(g.carry_max[0:1, :], g.run[0:1, 0, 1, :]).then_inc(s_st, 16)
            e.wait_ge(s_ld, 16 * NT)
            e.wait_ge(s_st, 48)


def prepare_edges(g):
    nc = g.nc
    s_fill, s_ld, s_chain, s_st, s_mat = (g.sem(n) for n in ("efill", "eload", "echain", "estore", "emat"))
    run, msg = g.flat(g.run, I32), g.flat(g.msg, I32)
    dst, before, rel = (run[:, c * STEPS:(c + 1) * STEPS] for c in range(3))
    relf = g.flat(g.run)[:, 3 * STEPS:4 * STEPS]
    dst_p, src_p, rel_p = (msg[:, c * PER:(c + 1) * PER] for c in range(3))
    pack = g.pack.rearrange("p (r a c) -> p r a c", a=2, c=ROW)
    with nc.Block() as block:
        @block.gpsimd
        def _(e):
            e.memset(run[:, 0:2 * STEPS], FAR).then_inc(s_fill, 1)
            e.memset(rel, 0).then_inc(s_fill, 1)
            e.memset(g.key_src[:, :], 0).then_inc(s_fill, 1)
            e.memset(g.key_rel[:, STEPS:], 0).then_inc(s_fill, 1)
            e.memset(dst_p, FAR).then_inc(s_fill, 1)
            e.memset(msg[:, PER:3 * PER], 0).then_inc(s_fill, 1)

        @block.sync
        def _(e):
            e.wait_ge(s_fill, 6)
            n = 0
            for ap, tile, width, first in ((g.dst, dst, STEPS, 0), (g.src, g.key_src[:, 0:STEPS], STEPS, 0),
                                           (g.rel, rel, STEPS, 0), (g.dst, dst_p, PER, 0), (g.src, src_p, PER, 0),
                                           (g.rel, rel_p, PER, 0), (g.dst, before[1:P, :], STEPS, STEPS - 1)):
                for out, part in edge_rows(ap, first, tile, width):
                    e.dma_start(out, part).then_inc(s_ld, 16)
                    n += 1
            e.dma_start(before[0:1, 1:STEPS], g.dst[0:STEPS - 1].rearrange("(a t) -> a t", a=1)).then_inc(s_ld, 16)
            g.loads = n + 1
            e.wait_ge(s_chain, 11)
            e.dma_start(g.edge_rows.rearrange("(p r) c -> p (r c)", p=P), g.pack[:, :]).then_inc(s_st, 16)
            e.wait_ge(s_st, 16)

        @block.vector
        def _(e):
            step = Chain(e, s_chain)
            e.wait_ge(s_ld, 16 * g.loads)
            step(e.tensor_tensor(g.keep_sum[:, :], dst, before, ALU.is_equal))
            step(e.tensor_reduce(g.whole[:, :], g.keep_sum[:, :], AX.X, ALU.min))
            step(e.memset(g.keep_sum[:, 0:1], 0.0))
            step(e.tensor_scalar(g.keep_max[:, :], g.keep_sum[:, :], BIG, -BIG, ALU.mult, ALU.add))
            step(e.tensor_scalar(relf, g.key_src[:, 0:STEPS], float(R), None, ALU.mult))
            step(e.tensor_tensor(g.key_rel[:, 0:STEPS], relf, rel, ALU.add))
            step(e.tensor_scalar(g.diag[:, 0, :], g.ident[:, :], g.whole[:, 0:1], None, ALU.mult))
            rows = "p (r c) -> p r c"
            step(e.tensor_copy(pack[:, :, 0, :], dst_p.rearrange(rows, c=ROW)))
            step(e.tensor_scalar(pack[:, :, 1, :], src_p.rearrange(rows, c=ROW), float(R), None, ALU.mult))
            step(e.tensor_tensor(pack[:, :, 1, :], pack[:, :, 1, :], rel_p.rearrange(rows, c=ROW), ALU.add))
            step(e.tensor_copy(g.firsts[:, :], pack[:, ::2, 0, 0]))

        @block.tensor
        def _(e):
            e.wait_ge(s_chain, 7)
            e.matmul(g.ps_t[:, 0, 0:P], g.ones[:, :], g.diag[:, 0, :], start=True, stop=True).then_inc(s_mat, 1)

    s_c = g.sem("chains")
    with nc.Block() as block:
        @block.vector
        def _(e):
            step = Chain(e, s_c)
            step(e.tensor_copy(g.chain_sum[:, :], g.ps_t[:, 0, 0:P]))
            step(e.tensor_scalar(g.chain_max[:, :], g.chain_sum[:, :], BIG, -BIG, ALU.mult, ALU.add))


def locate_nodes(g):
    nc = g.nc
    s_c, s_p, s_g = (g.sem(n) for n in ("lchain", "lprod", "lgather"))
    firsts, junk = g.Z2[:, 0:BLOCKS], g.Z2[:, BLOCKS:2 * BLOCKS]
    half = BLOCKS // 2
    near = g.CS.rearrange("p (j r a c) -> p j r a c", j=NT, r=2, a=2)
    cmp = g.flat(g.msg)[:, 0:NT * P]
    cmp4 = cmp.rearrange("p (j r c) -> p j r c", j=NT, r=2)
    cmp3 = cmp.rearrange("p (j c) -> p j c", j=NT)
    ends, begin, cnt, blk, t1, t2 = (g.small[:, c, :] for c in range(6))
    with nc.Block() as block:
        @block.vector
        def _(e):
            step = Chain(e, s_c)
            step(e.tensor_tensor(g.diag[:, :, :], g.ident[:, :].unsqueeze(1).to_broadcast([P, 7, P]),
                                 g.firsts[:, :].unsqueeze(2).to_broadcast([P, 7, P]), ALU.mult))
            e.wait_ge(s_p, 1)
            step(e.tensor_copy(firsts[:, 0:half], g.ps_out[:, 0, 0:half]))
            step(e.tensor_copy(firsts[:, half:], g.ps_out[:, 1, 0:half]))
            for j in range(NT):
                step(e.tensor_scalar(junk, firsts, g.node[:, j:j + 1], 0.0, ALU.is_le, ALU.add,
                                     accum_out=cnt[:, j:j + 1]))
            step(e.tensor_scalar(blk, cnt, -1.0, 0.0, ALU.add, ALU.max))
            step(e.tensor_copy(g.near_at[:, :], blk))
            e.wait_ge(s_g, 16 * NT)
            for r in range(2):
                step(e.tensor_tensor(cmp4[:, :, r, :], near[:, :, r, 0, :],
                                     g.node[:, :].unsqueeze(2).to_broadcast([P, NT, ROW]), ALU.is_le))
            step(e.tensor_reduce(cnt, cmp3, AX.X, ALU.add))
            step(e.tensor_scalar(blk, blk, float(2 * ROW), None, ALU.mult))
            step(e.tensor_tensor(ends, blk, cnt, ALU.add))
            step(e.memset(g.ends1[:, 0:1], 0.0))
            step(e.tensor_copy(g.ends1[:, 1:NT + 1], ends))
            e.wait_ge(s_p, 2)
            step(e.tensor_copy(begin, g.ps_t[:, 0, 0:NT]))
            step(e.tensor_tensor(g.degree[:, :], ends, begin, ALU.subtract))
            step(e.tensor_scalar(t1, g.degree[:, :], 0.0, None, ALU.is_gt))
            step(e.tensor_scalar(ends, ends, -1.0, None, ALU.add))
            step(e.tensor_tensor(cmp3, ends.unsqueeze(2).to_broadcast([P, NT, P]),
                                 g.block0[:, :].unsqueeze(1).to_broadcast([P, NT, P]), ALU.is_ge))
            step(e.tensor_reduce(blk, cmp3, AX.X, ALU.add))
            step(e.tensor_scalar(blk, blk, -1.0, None, ALU.add))
            step(e.tensor_scalar(t2, blk, float(STEPS), None, ALU.mult))
            step(e.tensor_tensor(t2, begin, t2, ALU.is_lt))
            step(e.tensor_tensor(blk, blk, t2, ALU.mult))
            step(e.tensor_tensor(g.carry_at[:, :], blk, t1, ALU.mult))
            step(e.tensor_scalar(ends, ends, float(-P * STEPS), None, ALU.add))
            step(e.tensor_tensor(ends, ends, t1, ALU.mult))
            step(e.tensor_scalar(g.last_at[:, :], ends, float(P * STEPS), None, ALU.add))

        @block.tensor
        def _(e):
            e.wait_ge(s_c, 1)
            flat = g.diag[:, :, :].rearrange("p a b -> p (a b)")
            e.matmul(g.ps_out[:, 0, 0:half], g.ones[:, :], flat[:, 0:half], start=True, stop=True)
            e.matmul(g.ps_out[:, 1, 0:half], g.ones[:, :], flat[:, half:], start=True, stop=True).then_inc(s_p, 1)
            e.wait_ge(s_c, NT + 12)
            e.matmul(g.ps_t[:, 0, 0:NT], g.shift[:, :], g.ends1[:, 1:NT + 1], start=True, stop=False)
            e.matmul(g.ps_t[:, 0, 0:NT], g.corner[:, :], g.ends1[:, 0:NT], start=False, stop=True).then_inc(s_p, 1)

        @block.gpsimd
        def _(e):
            e.wait_ge(s_c, NT + 5)
            blocks = g.edge_rows.rearrange("(b r) c -> b (r c)", r=2)
            for j in range(NT):
                e.indirect_dma_start(g.CS[:, j * 4 * ROW:(j + 1) * 4 * ROW], None, blocks,
                                     bass.IndirectOffsetOnAxis(g.near_at[:, j:j + 1], 0)).then_inc(s_g, 16)


def locate_windows(g):
    nc = g.nc
    s_c, s_p, s_g, s_d, s_e, s_v = (g.sem(n) for n in ("wchain", "wprod", "wgather", "wdma", "wcopy", "wvec"))
    begin = g.small[:, 1, :]
    found = g.flat(g.run)[:, 0:GROUPS * 4 * 2 * ROW].rearrange("p (g c a r) -> p g c a r", g=GROUPS, c=4, a=2)
    cs_d = g.CS[:, 0:WTILES * NW].rearrange("p (g r) -> p g r", g=GROUPS)
    cs_k = g.CS[:, WTILES * NW:2 * WTILES * NW].rearrange("p (g r) -> p g r", g=GROUPS)
    dst = g.flat(g.msg)[:, 0:WTILES * NW]
    key = g.flat(g.msg, I32)[:, WTILES * NW:2 * WTILES * NW]
    dst4 = dst.rearrange("p (q w g) -> p q w g", q=WTILES, g=GROUPS)
    key4 = key.rearrange("p (q w g) -> p q w g", q=WTILES, g=GROUPS)
    ti, tf, tg = g.CSI[:, 0:WTILES * NW], g.CS[:, WTILES * NW:2 * WTILES * NW], g.Z2[:, 0:WTILES * NW]
    low, spot = (x[:, :, :].rearrange("p q w -> p (q w)") for x in (g.low, g.spot))
    with nc.Block() as block:
        @block.tensor
        def _(e):
            e.transpose(g.ps_t[0:NT, 0, 0:P], begin, g.ident[:, :]).then_inc(s_p, 1)
            e.wait_ge(s_e, 2)
            n = 0
            for gr in range(GROUPS):
                if gr >= 2:
                    e.wait_ge(s_v, 2 * (gr - 1))
                for q in range(WTILES):
                    for x, src in enumerate((cs_d, cs_k)):
                        last = e.transpose(g.ps_t[:, gr % 2, (2 * x + q) * P:(2 * x + q + 1) * P],
                                           src[:, gr, q * P:(q + 1) * P], g.ident[:, :])
                last.then_inc(s_p, 1)

        @block.vector
        def _(e):
            step = Chain(e, s_c)
            e.wait_ge(s_p, 1)
            step(e.tensor_copy(g.wrow[0:NT, :], g.ps_t[0:NT, 0, 0:P:WIN]))
            step(e.tensor_scalar(g.wrow[0:NT, :], g.wrow[0:NT, :], ROW.bit_length() - 1, None, ALU.arith_shift_right))
            e.wait_ge(s_d, 48)
            for c in range(4):
                step(e.tensor_scalar(g.win_at[:, c, :], g.win_row[:, :], float(c), None, ALU.add))
            e.wait_ge(s_g, 16 * 4 * GROUPS)
            e.tensor_copy(cs_d.rearrange("p g (c r) -> p g c r", c=4), found[:, :, :, 0, :]).then_inc(s_e, 1)
            e.tensor_copy(cs_k.rearrange("p g (c r) -> p g c r", c=4), found[:, :, :, 1, :]).then_inc(s_e, 1)
            for gr in range(GROUPS):
                e.wait_ge(s_p, gr + 2)
                ps = g.ps_t[:, gr % 2, :].rearrange("p (x q w) -> p x q w", x=2, q=WTILES)
                e.tensor_copy(dst4[:, :, :, gr], ps[:, 0]).then_inc(s_v, 1)
                e.tensor_copy(key4[:, :, :, gr], ps[:, 1]).then_inc(s_v, 1)
            e.wait_ge(s_v, 2 * GROUPS)
            step(e.tensor_scalar(ti, key, R.bit_length() - 1, P - 1, ALU.arith_shift_right, ALU.bitwise_and))
            step(e.tensor_copy(low, ti))
            step(e.tensor_scalar(ti, key, (R * P).bit_length() - 1, None, ALU.arith_shift_right))
            step(e.tensor_tensor(g.spot[:, :, :], dst.rearrange("p (q w) -> p q w", q=WTILES),
                                 g.window0[:, :].unsqueeze(1).to_broadcast([P, WTILES, NW]), ALU.subtract))
            step(e.tensor_scalar(tf, spot, 0.0, float(WIN - 1), ALU.max, ALU.min))
            step(e.tensor_tensor(tg, tf, spot, ALU.is_equal))
            step(e.tensor_reduce(g.check[:, 0:1], tg, AX.X, ALU.add))
            step(e.scalar_tensor_tensor(spot, ti, float(WIN), spot, ALU.mult, ALU.add))
            step(e.scalar_tensor_tensor(spot, spot, 1.0, tg, ALU.add, ALU.mult))
            step(e.tensor_scalar(spot, spot, -1.0, None, ALU.add))

        @block.sync
        def _(e):
            flat = g.window_rows.rearrange("(j u) -> j u", u=P // WIN)
            e.dma_start(flat[NT:NW * WIN // P, :], g.past[0:NW * WIN // P - NT, 0:P // WIN]).then_inc(s_d, 16)
            e.wait_ge(s_c, 2)
            e.dma_start(flat[0:NT, :], g.wrow[0:NT, :]).then_inc(s_d, 16)
            e.wait_ge(s_d, 32)
            e.dma_start(g.win_row[:, :], g.window_rows.rearrange("(p g) -> p g", g=GROUPS)).then_inc(s_d, 16)
            e.wait_ge(s_d, 48)

        @block.gpsimd
        def _(e):
            e.wait_ge(s_c, 6)
            run = g.flat(g.run)
            for gr in range(GROUPS):
                for c in range(4):
                    at = (gr * 4 + c) * 2 * ROW
                    e.indirect_dma_start(run[:, at:at + 2 * ROW], None, g.edge_rows,
                                         bass.IndirectOffsetOnAxis(g.win_at[:, c, gr:gr + 1], 0)).then_inc(s_g, 16)


def layer_norm(g, gain=None, shift=None, relu=True):
    nc = g.nc
    s_chain, s_v, s_r = (g.sem(n) for n in ("nchain", "var", "dev"))
    src = g.X if gain is None else g.Y
    wide = [P, NT, D]
    with nc.Block() as block:
        @block.vector
        def _(e):
            step = Chain(e, s_chain)
            step(e.tensor_reduce(g.mean[:, :], src[:, :, :], AX.X, ALU.add))
            step(e.tensor_scalar(g.mean[:, :], g.mean[:, :], -1.0 / D, None, ALU.mult))
            step(e.tensor_tensor(g.H[:, :, :], src[:, :, :], g.mean[:, :].unsqueeze(2).to_broadcast(wide), ALU.add))
            step(e.tensor_tensor(g.Z[:, :, :], g.H[:, :, :], g.H[:, :, :], ALU.mult))
            step(e.tensor_reduce(g.var[:, :], g.Z[:, :, :], AX.X, ALU.add))
            e.tensor_scalar(g.var[:, :], g.var[:, :], 1.0 / D, 1e-5, ALU.mult, ALU.add).then_inc(s_v, 1)
            e.wait_ge(s_r, 1)
            step(e.reciprocal(g.mean[:, :], g.dev[:, :]))
            step(e.tensor_tensor(g.H[:, :, :], g.H[:, :, :], g.mean[:, :].unsqueeze(2).to_broadcast(wide), ALU.mult))
            if gain is not None:
                step(e.tensor_tensor(g.H[:, :, :], g.H[:, :, :], gain.unsqueeze(1).to_broadcast(wide), ALU.mult))
                step(e.tensor_tensor(g.H[:, :, :], g.H[:, :, :], shift.unsqueeze(1).to_broadcast(wide), ALU.add))
            if relu:
                step(e.tensor_scalar(g.H[:, :, :], g.H[:, :, :], 0.0, None, ALU.max))

        @block.scalar
        def _(e):
            e.wait_ge(s_v, 1)
            e.activation(g.dev[:, :], g.var[:, :], ACT.Sqrt).then_inc(s_r, 1)


def back(k):
    return 1 if k == 0 else 2


def project(g, src, weights, cols, evacuate, hidden=None, store=None):
    nc = g.nc
    s_in, s_T, s_hT, s_mm, s_ev, s_h1, s_h2 = (g.sem(n) for n in (
        "pin", "ptrans", "pcopy", "pprod", "pevac", "phid", "prelu"))
    s_st = [g.sem(f"pstore{i}") for i in range(2)]
    stages = [(c, min(c + 512, cols)) for c in range(0, cols, 512)]

    def body(e, f):
        with e.Fori(0, TROUNDS) as i:
            for k in range(TILES):
                f(i * TILES + k, k, k % 2)

    with nc.Block() as block:
        @block.scalar
        def _(e):
            def tile(n, k, s):
                e.wait_ge(s_T, n - back(k) + 3)
                e.activation(g.tin[:, s, :], src[:, bass.ds(n, 1), :].rearrange("p a f -> p (a f)"),
                             ACT.Copy).then_inc(s_in, 1)
                e.wait_ge(s_T, n + 3)
                e.wait_ge(s_mm, n - back(k) + 3)
                e.activation(g.tT[:, s, :], g.ps_t[:, s, 0:P], ACT.Copy).then_inc(s_hT, 1)
                if hidden:
                    e.wait_ge(s_h1, n + 1)
                    e.activation(g.tH[:, s, :], g.ps_t[:, s, P:2 * P], ACT.Relu, bias=hidden[1],
                                 scale=hidden[0]).then_inc(s_h2, 1)
            body(e, tile)

        @block.tensor
        def _(e):
            e.sem_inc(s_T, 2)
            e.sem_inc(s_mm, 2)

            def tile(n, k, s):
                e.wait_ge(s_in, n + 1)
                e.wait_ge(s_hT, n - back(k) + 3)
                e.transpose(g.ps_t[:, s, 0:P], g.tin[:, s, :], g.ident[:, :]).then_inc(s_T, 1)
                e.wait_ge(s_hT, n + 3)
                if hidden:
                    e.matmul(g.ps_t[:, s, P:2 * P], weights, g.tT[:, s, :], start=True, stop=True).then_inc(s_h1, 1)
                    e.wait_ge(s_h2, n + 1)
                rows, w = (g.tH, hidden[2]) if hidden else (g.tT, weights)
                e.wait_ge(s_ev, n - back(k) + 3)
                for a, b in stages:
                    last = e.matmul(g.ps_out[:, s, a:b], rows[:, s, :], w[:, a:b], start=True, stop=True)
                last.then_inc(s_mm, 1)
            body(e, tile)

        @block.vector
        def _(e):
            e.sem_inc(s_hT, 2)
            e.sem_inc(s_ev, 2)

            def tile(n, k, s):
                e.wait_ge(s_mm, n + 3)
                if store:
                    per, done = (3, (k + 1) // 2) if s == 0 else (2, k // 2)
                    e.wait_ge(s_st[s], (i_of(n, k) * per + done) * 16 + 16)
                evacuate(e, n, s).then_inc(s_ev, 1)

            def i_of(n, k):
                return rounds[0]
            rounds = [None]
            with e.Fori(0, TROUNDS) as i:
                rounds[0] = i
                for k in range(TILES):
                    tile(i * TILES + k, k, k % 2)

        if store:
            @block.sync
            def _(e):
                for s in range(2):
                    e.dma_start(g.credit[s:s + 1, :], g.ident[0:1, 0:1]).then_inc(s_st[s], 16)

                def tile(n, k, s):
                    e.wait_ge(s_ev, n + 3)
                    store(e, n, s).then_inc(s_st[s], 16)
                body(e, tile)
                e.wait_ge(s_st[0], 16 * (3 * TROUNDS + 1))
                e.wait_ge(s_st[1], 16 * (2 * TROUNDS + 1))


def aggregate(g, table, key, op, build=False):
    nc = g.nc
    adds = op == ALU.add
    keep, chain, carry = (g.keep_sum, g.chain_sum, g.carry_sum) if adds else (g.keep_max, g.chain_max, g.carry_max)
    join = ALU.mult if adds else ALU.add
    s_idx = [g.sem(f"idx{h}") for h in range(2)]
    s_msg = [g.sem(f"msg{h}") for h in range(2)]
    s_out = [g.sem(f"rout{h}") for h in range(2)]
    s_run, s_go = g.sem("run"), g.sem("go")
    s_hot, s_cnt, s_adj, s_max, s_sto, s_clr = (g.sem(n) for n in ("hot", "count", "adj", "most", "adjstore", "clear"))
    both = 2 * HALF
    ahead = both + 1
    running = g.running[0:P * STEPS, :].rearrange("(p t) f -> p t f", t=STEPS)

    def counts(k):
        return g.ps_out[:, (k % RING) // 2, (k % 2) * 512:(k % 2) * 512 + KW]

    with nc.Block() as block:
        @block.gpsimd
        def _(e):
            def indices(h, t):
                e.tensor_copy(g.idx[:, h, :], key[:, bass.ds(t, HALF)]).then_inc(s_idx[h], 1)

            indices(0, 0)
            with e.Fori(0, ROUNDS) as i:
                for h in range(2):
                    e.wait_ge(s_idx[h], i + 1)
                    e.sem_inc(s_go, 1)
                    for k in range(HALF):
                        if k == HALF - 2:
                            e.wait_ge(s_run, i * both + (h * HALF + ahead))
                            e.sem_inc(s_go, 1)
                            indices(1 - h, i * both + (h + 1) * HALF)
                        e.indirect_dma_start(g.msg[:, h, k, :], None, table,
                                             bass.IndirectOffsetOnAxis(g.idx[:, h, k:k + 1], 0)).then_inc(s_msg[h], 16)

        @block.vector
        def _(e):
            e.memset(g.run[:, 1, HALF - 1, :], 0.0 if adds else -BIG).then_inc(s_run, 1)
            e.sem_inc(s_run, both)
            if build:
                e.memset(g.most[:, :], 0.0).then_inc(s_max, 1)
                e.sem_inc(s_max, RING + 1)
            with e.Fori(0, ROUNDS) as i:
                for h in range(2):
                    e.wait_ge(s_msg[h], i * (16 * HALF) + 16 * HALF)
                    e.wait_ge(s_out[h], i * 16 + 16)
                    for k in range(HALF):
                        prev = g.run[:, h, k - 1, :] if k else g.run[:, 1 - h, HALF - 1, :]
                        u = h * HALF + k
                        t = i * both + u
                        e.wait_ge(s_run, t + ahead)
                        e.scalar_tensor_tensor(g.run[:, h, k, :], prev, keep[:, bass.ds(t, 1)], g.msg[:, h, k, :],
                                               join, op).then_inc(s_run, 1)
                        if not build:
                            continue
                        e.wait_ge(s_cnt, t + 1)
                        for q in range(WTILES):
                            e.tensor_scalar(g.hot_low[:, u % RING, q, :], g.iota_h[:, :], g.low[:, q, bass.ds(t, 1)],
                                            None, ALU.is_equal).then_inc(s_hot, 1)
                            e.tensor_scalar(g.hot_spot[:, u % RING, q, :], g.iota_h[:, 0:KW], g.spot[:, q, bass.ds(t, 1)],
                                            None, ALU.is_equal).then_inc(s_hot, 1)
                        e.wait_ge(s_adj, t + RING - 1)
                        e.wait_ge(s_max, t + RING + 2)
                        e.tensor_tensor(g.most[:, :], g.most[:, :], counts(u - 2), ALU.max).then_inc(s_max, 1)
            if build:
                for u in range(2):
                    e.wait_ge(s_adj, STEPS + RING - 1 + u)
                    e.wait_ge(s_max, STEPS + RING + 2 + u)
                    e.tensor_tensor(g.most[:, :], g.most[:, :], counts(STEPS - 2 + u), ALU.max).then_inc(s_max, 1)

        if build:
            @block.tensor
            def _(e):
                for u in (2, 1):
                    e.matmul(counts(RING - u), g.zero_h[:, :], g.zero_h[:, 0:KW], start=True, stop=True).then_inc(s_clr, 1)
                e.wait_ge(s_clr, 2)
                e.sem_inc(s_cnt, RING)
                with e.Fori(0, ROUNDS) as i:
                    for u in range(both):
                        t = i * both + u
                        e.wait_ge(s_hot, (t + 1) * (2 * WTILES))
                        e.wait_ge(s_adj, t + 1)
                        e.wait_ge(s_max, t + RING + 1)
                        for q in range(WTILES):
                            last = e.matmul(counts(u), g.hot_low[:, u % RING, q, :], g.hot_spot[:, u % RING, q, :],
                                            start=q == 0, stop=q == WTILES - 1)
                        last.then_inc(s_cnt, 1)

            @block.scalar
            def _(e):
                e.sem_inc(s_adj, RING)
                with e.Fori(0, ROUNDS) as i:
                    e.wait_ge(s_sto, i * 16 + 16)
                    e.sem_inc(s_go, 1)
                    for u in range(both):
                        e.wait_ge(s_cnt, i * both + (u + RING + 1))
                        e.sem_inc(s_go, 1)
                        e.activation(g.adj[:, :, u * WIN:(u + 1) * WIN],
                                     counts(u).rearrange("p (h n) -> p h n", n=WIN), ACT.Copy,
                                     saturate=False).then_inc(s_adj, 1)

        @block.sync
        def _(e):
            for h in range(2):
                e.dma_start(g.credit[h:h + 1, :], g.ident[0:1, 0:1]).then_inc(s_out[h], 16)
            if build:
                e.dma_start(g.credit[2:3, :], g.ident[0:1, 0:1]).then_inc(s_sto, 16)
            with e.Fori(0, ROUNDS) as i:
                for h in range(2):
                    e.wait_ge(s_run, i * both + (h + 1) * HALF + ahead)
                    e.dma_start(running[:, bass.ds(i * both + h * HALF, HALF), :],
                                g.run[:, h, :, :]).then_inc(s_out[h], 16)
                if build:
                    e.wait_ge(s_adj, i * both + (both + RING))
                    e.sem_inc(s_go, 1)
                    e.dma_start(g.adjacency[bass.ds(i, 1), :, :].rearrange("a p c -> (a p) c"),
                                g.adj[:, :, :].rearrange("p h n -> p (h n)").bitcast(U8)).then_inc(s_sto, 16)
            for h in range(2):
                e.wait_ge(s_out[h], 16 * (ROUNDS + 1))
            if build:
                e.wait_ge(s_sto, 16 * (ROUNDS + 1))

    s_t, s_s, s_c, s_d, s_a = (g.sem(n) for n in ("ctrans", "cscan", "ccopy", "cstore", "agather"))
    with nc.Block() as block:
        @block.gpsimd
        def _(e):
            for j in range(NT):
                e.indirect_dma_start(g.Z[:, j, :], None, g.running,
                                     bass.IndirectOffsetOnAxis(g.last_at[:, j:j + 1], 0)).then_inc(s_a, 16)
            e.wait_ge(s_d, 16)
            for j in range(NT):
                e.indirect_dma_start(g.C[:, j, :], None, carry,
                                     bass.IndirectOffsetOnAxis(g.carry_at[:, j:j + 1], 0)).then_inc(s_a, 16)

        @block.tensor
        def _(e):
            e.transpose(g.ps_t[:, 0, 0:P], g.run[:, 1, HALF - 1, :], g.ident[:, :]).then_inc(s_t, 1)
            e.wait_ge(s_s, 1)
            e.transpose(g.ps_t[:, 1, 0:P], g.tT[:, 0, :], g.ident[:, :]).then_inc(s_t, 1)

        @block.vector
        def _(e):
            e.wait_ge(s_t, 1)
            e.tensor_tensor_scan(g.tT[:, 0, :], chain[:, :], g.ps_t[:, 0, 0:P], 0.0 if adds else -BIG,
                                 join, op).then_inc(s_s, 1)
            e.wait_ge(s_t, 2)
            e.tensor_copy(g.tT[:, 1, :], g.ps_t[:, 1, 0:P]).then_inc(s_c, 1)
            e.wait_ge(s_a, 32 * NT)
            e.tensor_tensor(g.Z[:, :, :], g.Z[:, :, :], g.C[:, :, :], op)

        @block.sync
        def _(e):
            e.wait_ge(s_c, 1)
            e.dma_start(carry[1:P + 1, :], g.tT[:, 1, :]).then_inc(s_d, 16)
            e.wait_ge(s_d, 16)


def check_adjacency(g):
    nc = g.nc
    s_c, s_p = g.sem("kchain"), g.sem("kprod")
    with nc.Block() as block:
        @block.vector
        def _(e):
            step = Chain(e, s_c)
            step(e.tensor_reduce(g.check[:, 1:2], g.most[:, :], AX.X, ALU.max))
            e.wait_ge(s_p, 1)
            step(e.tensor_copy(g.check[0:1, 2:3], g.ps_t[0:1, 0, 0:1]))
            step(e.tensor_reduce(g.check[0:1, 3:4], g.ps_t[0:1, 1, 0:P], AX.X, ALU.max))
            step(e.tensor_scalar(g.check[0:1, 2:3], g.check[0:1, 2:3], float(E), None, ALU.not_equal))
            step(e.tensor_scalar(g.check[0:1, 3:4], g.check[0:1, 3:4], float(EXACT), None, ALU.is_gt))
            step(e.tensor_tensor(g.flag[:, :], g.check[0:1, 2:3], g.check[0:1, 3:4], ALU.max))

        @block.tensor
        def _(e):
            e.wait_ge(s_c, 1)
            e.matmul(g.ps_t[0:1, 0, 0:1], g.check[:, 0:1], g.ones[:, 0:1], start=True, stop=True)
            e.transpose(g.ps_t[0:1, 1, 0:P], g.check[:, 1:2], g.ident[:, :]).then_inc(s_p, 1)


def multiply(g, src, scale):
    nc = g.nc
    s_c, s_go, s_mm, s_lo, s_ev = (g.sem(n) for n in ("cut", "mgo", "mprod", "mlow", "mevac"))
    s_ld = [g.sem(f"mload{k}") for k in range(TILES)]
    with nc.Block() as block:
        @block.gpsimd
        def _(e):
            e.sem_inc(s_go, 1)

        @block.sync
        def _(e):
            with e.Fori(0, TROUNDS) as i:
                for k in range(TILES):
                    e.wait_ge(s_mm, i * TILES + k + 1)
                    e.sem_inc(s_go, 1)
                    e.dma_start(g.adj_in[:, k, :], g.adjacency[bass.ds(i * TILES + k, 1), :, :].rearrange(
                        "a p c -> (a p) c")).then_inc(s_ld[k], 16)

        @block.vector
        def _(e):
            e.tensor_scalar(g.cut[:, :, 0, :], src[:, :, :], scale[0], None, ALU.mult).then_inc(s_c, 1)
            e.wait_ge(s_c, 1)
            e.scalar_tensor_tensor(g.cut[:, :, 1, :], src[:, :, :], scale[0], g.cut[:, :, 0, :],
                                   ALU.mult, ALU.subtract).then_inc(s_c, 1)
            e.sem_inc(s_ev, 2)
            with e.Fori(0, TROUNDS) as i:
                for k in range(TILES):
                    n = i * TILES + k
                    e.wait_ge(s_lo, n + 1)
                    e.scalar_tensor_tensor(g.Z[:, bass.ds(n, 1), :].rearrange("p a f -> p (a f)"),
                                           g.ps_out[:, k % 2, 0:D], scale[1], g.tin[:, k % 2, :],
                                           ALU.mult, ALU.add).then_inc(s_ev, 1)

        @block.scalar
        def _(e):
            with e.Fori(0, TROUNDS) as i:
                for k in range(TILES):
                    n = i * TILES + k
                    e.wait_ge(s_mm, n + TILES + 1)
                    e.wait_ge(s_ev, n - back(k) + 3)
                    e.activation(g.tin[:, k % 2, :], g.ps_out[:, k % 2, D:2 * D], ACT.Copy,
                                 scale=scale[1]).then_inc(s_lo, 1)

        @block.tensor
        def _(e):
            e.sem_inc(s_mm, TILES)
            e.wait_ge(s_c, 2)
            with e.Fori(0, TROUNDS) as i:
                for k in range(TILES):
                    n = i * TILES + k
                    e.wait_ge(s_ld[k], i * 16 + 16)
                    e.wait_ge(s_ev, n - back(k) + 3)
                    e.sem_inc(s_go, 1)
                    adj = g.adj_in[:, k, :].bitcast(F8).rearrange("p (h n) -> p h n", h=NT)
                    for t in range(NT):
                        last = e.matmul(g.ps_out[:, k % 2, 0:2 * D], adj[:, t, :],
                                        g.cut[:, t, :, :].rearrange("p a f -> p (a f)"),
                                        start=t == 0, stop=t == NT - 1)
                    last.then_inc(s_mm, 1)


def neighbours(g, src, scale):
    flag = g.nc.values_load(g.flag[0:1, 0:1], min_val=0, max_val=1,
                            skip_runtime_bounds_check_because="it is the result of comparisons")
    with g.nc.If(flag):
        store_rows(g, src)
        aggregate(g, g.table1, g.key_src, ALU.add)
    with g.nc.Else():
        multiply(g, src, scale)
    g.nc.end_all_ifs()


def find_scale(g, src):
    nc = g.nc
    s_c, s_p = g.sem("uchain"), g.sem("uprod")
    with nc.Block() as block:
        @block.vector
        def _(e):
            step = Chain(e, s_c)
            step(e.tensor_reduce(g.unit[:, 2:3], src[:, :, :], AX.XY, ALU.max, apply_absolute_value=True))
            e.wait_ge(s_p, 1)
            step(e.tensor_reduce(g.unit[0:1, 3:4], g.ps_t[0:1, 0, 0:P], AX.X, ALU.max))
            step(e.tensor_scalar(g.unit[0:1, 4:5], g.unit[0:1, 3:4], 1e-30, 1.0 / TOP, ALU.max, ALU.mult))
            step(e.reciprocal(g.unit[0:1, 3:4], g.unit[0:1, 4:5]))
            e.wait_ge(s_p, 2)
            step(e.tensor_copy(g.unit[:, 0:2], g.ps_t[:, 1, 0:2]))

        @block.tensor
        def _(e):
            e.wait_ge(s_c, 1)
            e.transpose(g.ps_t[0:1, 0, 0:P], g.unit[:, 2:3], g.ident[:, :]).then_inc(s_p, 1)
            e.wait_ge(s_c, 4)
            e.matmul(g.ps_t[:, 1, 0:2], g.ones[0:1, :], g.unit[0:1, 3:5], start=True, stop=True).then_inc(s_p, 1)


def load_params(g, pairs):
    s_w = g.sem("params")
    with g.nc.Block() as block:
        @block.sync
        def _(e):
            for out, part in pairs:
                e.dma_start(out, part).then_inc(s_w, 16)
            e.wait_ge(s_w, 16 * len(pairs))


def row(ap):
    return ap.rearrange("(a n) -> a n", a=1).to_broadcast([P, ap.shape[0]])


def vector_stage(g, f):
    s = g.sem("vstage")
    with g.nc.Block() as block:
        @block.vector
        def _(e):
            f(e, Chain(e, s))


def relational(g, table):
    def evacuate(e, n, s):
        e.tensor_tensor(g.stage[:, s, 0:512], g.ps_out[:, s, 0:512], g.bias9[:, 0:512], ALU.add)
        e.tensor_tensor(g.S[:, bass.ds(n, 1), :].rearrange("p a f -> p (a f)"), g.ps_out[:, s, R * D:W9],
                        g.bias9[:, R * D:W9], ALU.add)
        return e.tensor_tensor(g.stage[:, s, 512:1024], g.ps_out[:, s, 512:1024], g.bias9[:, 512:1024], ALU.add)

    def store(e, n, s):
        return e.dma_start(table.rearrange("(m p r) f -> p m (r f)", p=P, r=R)[:, bass.ds(n, 1), :].rearrange(
            "p a f -> p (a f)"), g.stage[:, s, :])
    project(g, g.H, g.w9, W9, evacuate, store=store)


def store_rows(g, src):
    s = g.sem("rows")
    with g.nc.Block() as block:
        @block.sync
        def _(e):
            e.dma_start(g.table1.rearrange("(j p) f -> p j f", p=P), src[:, :, :]).then_inc(s, 16)
            e.wait_ge(s, 16)


def gnn_kernel(nc, a, out):
    with ExitStack() as ctx:
        g = Program(nc, ctx)
        g.x, g.src, g.dst, g.rel = (a[n] for n in ("x", "src", "dst", "edge_type_8"))
        g.running = g.dram("running_rows", [P * STEPS + 1, D])
        g.carry_sum = g.dram("carry_rows_sum", [P + 1, D])
        g.carry_max = g.dram("carry_rows_max", [P + 1, D])
        g.table8 = g.dram("table_rel", [NP * R, D])
        g.table1 = g.dram("table_node", [NP, D])
        g.edge_rows = g.dram("edge_rows", [P * PER // ROW, 2 * ROW])
        g.window_rows = g.dram("window_rows", [NW], I32)
        g.adjacency = g.dram("adjacency", [NT, P, NT * P], U8)
        g.credit = g.dram("credit", [3, 1])
        g.X, g.H, g.Z = (g.sb(n, [P, NT, D]) for n in "XHZ")
        cs = g.sb("CS", [P, 2, NT, D])
        g.C = g.Y = cs[:, 0]
        g.S = cs[:, 1]
        g.CS = cs[:, :, :, :].rearrange("p a j f -> p (a j f)")
        g.CSI = g.CS.bitcast(I32)
        g.Z2 = g.Z[:, :, :].rearrange("p j f -> p (j f)")
        g.mean, g.var, g.dev, g.degree, g.dis = (g.sb(n, [P, NT]) for n in ("mean", "var", "dev", "degree", "dis"))
        g.carry_at, g.last_at = (g.sb(n, [P, NT], I32) for n in ("carry_at", "last_at"))
        g.ident, g.shift, g.corner, g.ones, g.block0 = (g.sb(n, [P, P]) for n in ("ident", "shift", "corner", "ones", "block0"))
        g.chain_sum, g.chain_max = (g.sb(n, [P, P]) for n in ("chain_sum", "chain_max"))
        g.iota_i, g.iota_h = g.sb("iota_i", [P, 2 * P + NT], I32), g.sb("iota_h", [P, P], F16)
        g.iota_w, g.window0 = g.sb("iota_w", [P, NW], I32), g.sb("window0", [P, NW])
        g.past, g.wrow = (g.sb(n, [P, P // WIN], I32) for n in ("past", "wrow"))
        g.win_row, g.win_at = g.sb("win_row", [P, GROUPS], I32), g.sb("win_at", [P, 4, GROUPS], I32)
        g.near_at, g.node = g.sb("near_at", [P, NT], I32), g.sb("node", [P, NT])
        g.small, g.ends1 = g.sb("small", [P, 6, NT]), g.sb("ends1", [P, NT + 1])
        g.whole, g.firsts, g.diag = g.sb("whole", [P, 1]), g.sb("firsts", [P, 7]), g.sb("diag", [P, 7, P])
        g.pack = g.Y[:, :, :].rearrange("p j f -> p (j f)")[:, 0:2 * PER]
        g.low, g.spot = (g.sb(n, [P, WTILES, NW]) for n in ("low", "spot"))
        g.hot_low, g.hot_spot = g.sb("hot_low", [P, RING, WTILES, P], F16), g.sb("hot_spot", [P, RING, WTILES, KW], F16)
        g.zero_h, g.most = g.sb("zero_h", [P, P], F16), g.sb("most", [P, KW])
        g.adj, g.adj_in = g.sb("adj", [P, NT, P], F8), g.sb("adj_in", [P, TILES, NT * P], U8)
        g.cut = g.sb("cut", [P, NT, 2, D], F16)
        g.check, g.flag, g.unit = g.sb("check", [P, 4]), g.sb("flag", [1, 1], I32), g.sb("unit", [P, 5])
        g.key_src, g.key_rel = (g.sb(n, [P, STEPS + HALF], I32) for n in ("key_src", "key_rel"))
        g.keep_sum, g.keep_max = (g.sb(n, [P, STEPS]) for n in ("keep_sum", "keep_max"))
        g.idx = g.sb("idx", [P, 2, HALF], I32)
        g.msg, g.run = (g.sb(n, [P, 2, HALF, D]) for n in ("msg", "run"))
        g.tin, g.tT, g.tH = (g.sb(n, [P, 2, D]) for n in ("tin", "tT", "tH"))
        g.stage = g.sb("stage", [P, 2, R * D])
        g.w9, g.bias9 = g.sb("w9", [P, W9]), g.sb("bias9", [P, W9])
        g.rows = g.sb("rows", [P, 4, D])
        g.cols = g.sb("cols", [P, 8])
        g.ps_t = ctx.enter_context(nc.psum_tensor("ps_t", [P, 2, 512], F32))
        g.ps_out = ctx.enter_context(nc.psum_tensor("ps_out", [P, 2, 1536], F32))

        load_nodes_and_constants(g)
        prepare_edges(g)
        locate_nodes(g)
        locate_windows(g)

        load_params(g, [(g.w9[:, :].rearrange("k (r o) -> k r o", o=D),
                         a["L0_gnn_weight"].rearrange("r k o -> k r o")),
                        (g.bias9[:, :], row(a["L0_gnn_bias"].rearrange("r o -> (r o)")))])
        layer_norm(g)
        relational(g, g.table8)
        aggregate(g, g.table8, g.key_rel, ALU.max, build=True)
        check_adjacency(g)

        def finish0(e, step):
            step(e.tensor_tensor(g.Z[:, :, :], g.Z[:, :, :], g.S[:, :, :], ALU.add))
            step(e.scalar_tensor_tensor(g.X[:, :, :], g.Z[:, :, :], 0.0, g.X[:, :, :], ALU.max, ALU.add))
        vector_stage(g, finish0)

        g.recycle()

        load_params(g, [(g.w9[:, 0:D], a["L1_gnn_W1"]), (g.w9[:, D:2 * D], a["L1_gnn_W2"]),
                        (g.rows[:, 0, :], row(a["L1_gnn_b2"]))] +
                       [(g.cols[:, c:c + 1], a[f"L1_gnn_{n}"].rearrange("(p a) -> p a", a=1))
                        for c, n in enumerate(("b1", "gamma", "beta", "mov_mean", "mov_var"))])
        layer_norm(g)
        neighbours(g, g.H, (1024.0, 1.0 / 1024.0))
        s_v, s_r, s_n = g.sem("bnv"), g.sem("bnr"), g.sem("bnc")
        with nc.Block() as block:
            @block.vector
            def _(e):
                step = Chain(e, s_n)
                e.tensor_scalar(g.cols[:, 4:5], g.cols[:, 4:5], 0.001, None, ALU.add).then_inc(s_v, 1)
                step(e.tensor_tensor(g.Z[:, :, :], g.Z[:, :, :], g.H[:, :, :], ALU.add))
                step(e.tensor_tensor(g.cols[:, 0:1], g.cols[:, 0:1], g.cols[:, 3:4], ALU.subtract))
                e.wait_ge(s_r, 1)
                step(e.reciprocal(g.cols[:, 5:6], g.cols[:, 6:7]))
                step(e.tensor_tensor(g.cols[:, 5:6], g.cols[:, 5:6], g.cols[:, 1:2], ALU.mult))
                step(e.tensor_tensor(g.cols[:, 7:8], g.cols[:, 0:1], g.cols[:, 5:6], ALU.mult))
                step(e.tensor_tensor(g.cols[:, 7:8], g.cols[:, 7:8], g.cols[:, 2:3], ALU.add))

            @block.scalar
            def _(e):
                e.wait_ge(s_v, 1)
                e.activation(g.cols[:, 6:7], g.cols[:, 4:5], ACT.Sqrt).then_inc(s_r, 1)

        def evacuate1(e, n, s):
            return e.tensor_tensor(g.S[:, bass.ds(n, 1), :].rearrange("p a f -> p (a f)"), g.ps_out[:, s, 0:D],
                                   g.rows[:, 0, :], ALU.add)
        project(g, g.Z, g.w9[:, 0:D], D, evacuate1, hidden=(g.cols[:, 5:6], g.cols[:, 7:8], g.w9[:, D:2 * D]))

        def finish1(e, step):
            step(e.scalar_tensor_tensor(g.X[:, :, :], g.S[:, :, :], 0.0, g.X[:, :, :], ALU.max, ALU.add))
        vector_stage(g, finish1)

        g.recycle()

        for n, first in (("1", True), ("2", False)):
            load_params(g, [(g.w9[:, 0:R * D].rearrange("k (r o) -> k r o", o=D), a[f"L2_gnn_W{n}"].rearrange("r k o -> k r o")),
                            (g.w9[:, R * D:W9], a[f"L2_gnn_loop_w{n}"]),
                            (g.bias9[:, R * D:W9], row(a[f"L2_gnn_b{n}"]))])
            if first:
                layer_norm(g)

                def clear(e, step):
                    step(e.memset(g.bias9[:, 0:R * D], 0.0))
                vector_stage(g, clear)
            relational(g, g.table8)
            aggregate(g, g.table8, g.key_rel, ALU.add)

            def finish2(e, step):
                step(e.tensor_tensor(g.Z[:, :, :], g.Z[:, :, :], g.S[:, :, :], ALU.add))
                if first:
                    step(e.tensor_scalar(g.H[:, :, :], g.Z[:, :, :], 0.0, None, ALU.max))
                else:
                    step(e.tensor_tensor(g.X[:, :, :], g.Z[:, :, :], g.X[:, :, :], ALU.add))
            vector_stage(g, finish2)

        g.recycle()

        layer_norm(g)
        load_params(g, [(g.w9[:, 0:D], a["L3_gnn_W_in"]), (g.rows[:, 0, :], row(a["L3_gnn_b_in"]))])
        s_v, s_r, s_n = g.sem("gv"), g.sem("gr"), g.sem("gc")
        with nc.Block() as block:
            @block.vector
            def _(e):
                e.tensor_scalar(g.var[:, :], g.degree[:, :], 1.0, None, ALU.add).then_inc(s_v, 1)
                e.wait_ge(s_r, 1)
                e.reciprocal(g.dis[:, :], g.dev[:, :]).then_inc(s_n, 1)

            @block.scalar
            def _(e):
                e.wait_ge(s_v, 1)
                e.activation(g.dev[:, :], g.var[:, :], ACT.Sqrt).then_inc(s_r, 1)

        def evacuate_in(e, n, s):
            return e.tensor_tensor(g.S[:, bass.ds(n, 1), :].rearrange("p a f -> p (a f)"), g.ps_out[:, s, 0:D],
                                   g.rows[:, 0, :], ALU.add)
        project(g, g.H, g.w9[:, 0:D], D, evacuate_in)

        def to_h(e, step):
            step(e.tensor_copy(g.H[:, :, :], g.S[:, :, :]))
        vector_stage(g, to_h)
        for i in range(4):
            load_params(g, [(g.w9[:, 0:D], a["L3_gnn_Wc"][i]), (g.rows[:, 0, :], row(a["L3_gnn_bc"][i])),
                            (g.rows[:, 1, :], row(a["L3_gnn_ln_g"][i])), (g.rows[:, 2, :], row(a["L3_gnn_ln_b"][i]))])

            def evacuate_t(e, n, s):
                return e.tensor_scalar(g.S[:, bass.ds(n, 1), :].rearrange("p a f -> p (a f)"), g.ps_out[:, s, 0:D],
                                       g.dis[:, bass.ds(n, 1)], None, ALU.mult)
            project(g, g.H, g.w9[:, 0:D], D, evacuate_t)
            find_scale(g, g.S)
            neighbours(g, g.S, (g.unit[:, 0:1], g.unit[:, 1:2]))

            def combine(e, step):
                wide = [P, NT, D]
                step(e.tensor_tensor(g.Z[:, :, :], g.Z[:, :, :], g.S[:, :, :], ALU.add))
                step(e.tensor_tensor(g.Z[:, :, :], g.Z[:, :, :], g.dis[:, :].unsqueeze(2).to_broadcast(wide), ALU.mult))
                step(e.tensor_tensor(g.Z[:, :, :], g.Z[:, :, :], g.rows[:, 0, :].unsqueeze(1).to_broadcast(wide), ALU.add))
                step(e.scalar_tensor_tensor(g.Y[:, :, :], g.Z[:, :, :], 0.0, g.H[:, :, :], ALU.max, ALU.add))
            vector_stage(g, combine)
            layer_norm(g, g.rows[:, 1, :], g.rows[:, 2, :], relu=False)
            g.recycle()

        def finish3(e, step):
            step(e.tensor_tensor(g.X[:, :, :], g.X[:, :, :], g.H[:, :, :], ALU.add))
        vector_stage(g, finish3)
        s_o = g.sem("out")
        with nc.Block() as block:
            @block.sync
            def _(e):
                e.dma_start(out[0:N - LAST, :].rearrange("(j p) f -> p j f", p=P), g.X[:, 0:NT - 1, :]).then_inc(s_o, 16)
                e.dma_start(out[N - LAST:N, :], g.X[0:LAST, NT - 1, :]).then_inc(s_o, 16)
                e.wait_ge(s_o, 32)


def kernel(**inputs):
    import concourse.bacc as bacc
    from concourse.bass_utils import run_bass_kernel_spmd

    nc = bacc.Bacc("TRN2", target_bir_lowering=False, num_devices=1)
    arrays, aps = {}, {}
    for name, value in inputs.items():
        value = np.ascontiguousarray(value)
        arrays[f"in_{name}"] = value
        aps[name] = nc.dram_tensor(f"in_{name}", value.shape, mybir.dt.from_np(value.dtype), kind="ExternalInput").ap()
    out = nc.dram_tensor("out_x", (N, D), F32, kind="ExternalOutput").ap()
    gnn_kernel(nc, aps, out)
    return run_bass_kernel_spmd(nc, [arrays], core_ids=[0]).results[0]["out_x"]
```

```python
from contextlib import ExitStack

import numpy as np
import concourse.bass as bass
from concourse import mybir

F32, F16, BF16, F8 = mybir.dt.float32, mybir.dt.float16, mybir.dt.bfloat16, mybir.dt.float8e4
I32, U8 = mybir.dt.int32, mybir.dt.uint8
ALU = mybir.AluOpType
ACT = mybir.ActivationFunctionType
AX = mybir.AxisListType

P = 128
N = 3125
E = 100000
D = 128
R = 8
NT = -(-N // P)
NP = NT * P
LAST = N - (NT - 1) * P
WIN = 2
PAIR = 2
HALF = P // (WIN * PAIR) // 2
ROUNDS = NT
STEPS = ROUNDS * 2 * HALF
GROUP = 4
NG = 2 * HALF // GROUP
PER = 7 * P
BLOCKS = PER
SHIFT = 16
STARTS = E // SHIFT + 1
GROUPS = 13
NW = P * GROUPS
KW = NT * R * WIN
HD = P // 2
RING = 4
FAR = 5000
COUNT = 16.0
PIECES = [(0, 7), (7, 13), (13, 19), (19, 25)]
TILES = 5
TROUNDS = NT // TILES
EARLY_ROUNDS, EARLY_HALVES = 2, 1
BESIDE = 7
W9 = (R + 1) * D
BIG = 3.0e38
ALL = COUNT * E
TOP = 16384.0
assert P * STEPS >= E and P * PER >= STARTS * SHIFT + P and NW * WIN >= NP and TROUNDS * TILES == NT
assert PIECES[-1][1] == NT and len(PIECES) * GROUP == HALF and SHIFT == 16


class Chain:

    def __init__(self, eng, sem):
        self.eng, self.sem, self.n = eng, sem, 0

    def __call__(self, ins):
        self.n += 1
        ins.then_inc(self.sem, 1)
        self.eng.wait_ge(self.sem, self.n)


class Program:
    def __init__(self, nc, ctx):
        self.nc, self.ctx, self.count, self.sems = nc, ctx, 0, []

    def sb(self, name, shape, dt=F32):
        return self.ctx.enter_context(self.nc.sbuf_tensor(name, shape, dt))

    def sem(self, name):
        self.count += 1
        self.sems.append(self.nc.alloc_semaphore(f"{name}_{self.count}"))
        return self.sems[-1]

    def recycle(self):
        self.nc.clear_and_free_semaphores(self.sems)
        self.nc.all_engine_barrier()
        self.sems = []

    @staticmethod
    def flat(tile, dt=F32):
        row = tile.rearrange("p a b c -> p (a b c)")
        return row if dt == F32 else row.bitcast(dt)

    def dram(self, name, shape, dt=F32):
        return self.nc.dram_tensor(name, shape, dt).ap()


def edge_rows(ap, first, tile, width):
    whole = (E - first) // width
    rest = E - first - whole * width
    yield tile[0:whole, :], ap[first:first + whole * width].rearrange("(p t) -> p t", t=width)
    if rest:
        yield tile[whole:whole + 1, 0:rest], ap[first + whole * width:E].rearrange("(a t) -> a t", a=1)


def split_bias(g, step, e):
    rest, part, parts = g.arena[0:3, 0:W9], g.arena[0:3, W9:2 * W9].bitcast(BF16)[:, 0:W9], g.bias_parts[0:3, :]
    step(e.tensor_copy(rest, g.bias9[0:3, :]))
    step(e.memset(parts, 0.0))
    for k in range(3):
        step(e.tensor_copy(part, rest))
        step(e.scalar_tensor_tensor(parts, part, g.ident[0:3, k:k + 1], parts, ALU.mult, ALU.add))
        if k < 2:
            step(e.tensor_tensor(rest, rest, part, ALU.subtract))


def prepare(g, params):
    nc = g.nc
    s_fill, s_iota, s_sel, s_const, s_x, s_w, s_neutral = (g.sem(n) for n in (
        "fill", "iota", "select", "const", "xload", "params", "neutral"))
    s_pad, s_ld, s_chain, s_st, s_mat = (g.sem(n) for n in ("pad", "eload", "echain", "estore", "emat"))
    s_parts, s_bias = g.sem("parts"), g.sem("bias")
    run, msg = g.flat(g.run, I32), g.flat(g.msg, I32)
    dst, before, rel = (run[:, c * STEPS:(c + 1) * STEPS] for c in range(3))
    relf = g.flat(g.run)[:, 3 * STEPS:4 * STEPS]
    dst_p, src_p, rel_p = (msg[:, c * PER:(c + 1) * PER] for c in range(3))
    pack = g.Y[:, :, :].rearrange("p j f -> p (j f)")
    dstf, keyf = pack[:, 0:PER], pack[:, PER:2 * PER]
    neutral = g.tin
    listed, all_steps = 6, 11
    norm = Norm(g, g.X)
    loads = [pair for ap, tile, width, first in (
        (g.dst, dst, STEPS, 0), (g.src, g.key_src[:, 0:STEPS], STEPS, 0), (g.rel, rel, STEPS, 0),
        (g.dst, before[1:P, :], STEPS, STEPS - 1), (g.dst, dst_p, PER, 0), (g.src, src_p, PER, 0),
        (g.rel, rel_p, PER, 0)) for pair in edge_rows(ap, first, tile, width)]
    loads.append((before[0:1, 1:STEPS], g.dst[0:STEPS - 1].rearrange("(a t) -> a t", a=1)))

    def load_x(e, first, end):
        with e.Fori(first, end) as j:
            e.dma_start(g.X[:, bass.ds(j, 1), :].rearrange("p a f -> p (a f)"),
                        g.x[bass.ds(j * P, P), :]).then_inc(s_x, 16)

    with nc.Block() as block:
        @block.gpsimd
        def _(e):
            e.memset(run[:, 0:2 * STEPS], FAR).then_inc(s_pad, 1)
            e.memset(rel, 0).then_inc(s_pad, 1)
            e.memset(g.key_src[:, :], 0).then_inc(s_pad, 1)
            e.memset(g.key_rel[:, STEPS:], 0).then_inc(s_pad, 1)
            e.memset(dst_p, FAR).then_inc(s_pad, 1)
            e.memset(msg[:, PER:3 * PER], 0).then_inc(s_pad, 1)
            e.memset(g.ident[:, :], 0.0).then_inc(s_fill, 1)
            e.memset(g.ones[:, :], 1.0).then_inc(s_fill, 1)
            e.memset(neutral[:, 0, :], 0.0).then_inc(s_fill, 1)
            for m in (g.shift, g.corner):
                e.memset(m[:, :], 0.0).then_inc(s_fill, 1)
            e.memset(g.past[:, :], E // SHIFT).then_inc(s_fill, 1)
            e.wait_ge(s_fill, 6)
            e.affine_select(out=g.shift[:, :], in_=g.shift[:, :], compare_op=ALU.not_equal, fill=1.0,
                            base=-1, pattern=[[1, P]], channel_multiplier=-1).then_inc(s_sel, 1)
            e.affine_select(out=g.corner[:, :], in_=g.corner[:, :], compare_op=ALU.not_equal, fill=1.0,
                            base=P - 1, pattern=[[1, P]], channel_multiplier=-1).then_inc(s_sel, 1)
            e.affine_select(out=g.ident[:, :], in_=g.ident[:, :], compare_op=ALU.not_equal, fill=1.0,
                            base=0, pattern=[[-1, P]], channel_multiplier=1).then_inc(s_sel, 1)
            e.iota(g.iota_i[:, 0:KW], pattern=[[1, KW]], base=0, channel_multiplier=0).then_inc(s_iota, 1)
            e.iota(g.iota_i[:, KW:KW + P], pattern=[[STEPS, P]], base=0, channel_multiplier=0).then_inc(s_iota, 1)
            e.iota(g.iota_i[:, KW + P:KW + P + NT], pattern=[[P, NT]], base=0, channel_multiplier=1).then_inc(s_iota, 1)

        @block.sync
        def _(e):
            e.dma_start(*params[0]).then_inc(s_bias, 16)
            load_x(e, 0, NT // 2)
            e.wait_ge(s_const, 1)
            e.dma_start(g.X[0:LAST, NT - 1, :], g.x[N - LAST:N, :]).then_inc(s_x, 16)
            e.wait_ge(s_fill, 3)
            e.dma_start(g.running[P * STEPS:P * STEPS + 1, :], neutral[0:1, 0, :]).then_inc(s_neutral, 16)
            for out, part in params[1:]:
                e.dma_start(out, part).then_inc(s_w, 16)
            e.wait_ge(s_chain, listed)
            for k, part in enumerate((dstf, keyf)):
                e.dma_start(g.edge_list[k].rearrange("(p t) -> p t", p=P), part).then_inc(s_st, 16)
            e.wait_ge(s_st, 32)
            e.wait_ge(s_neutral, 16)
            e.wait_ge(s_w, 16 * len(params) - 16)

        @block.scalar
        def _(e):
            load_x(e, NT // 2, NT - 1)
            e.wait_ge(s_pad, 6)
            for out, part in loads:
                e.dma_start(out, part).then_inc(s_ld, 16)
            norm.scalar(e)

        @block.vector
        def _(e):
            e.memset(g.X[:, NT - 1, :], 0.0).then_inc(s_const, 1)
            e.memset(g.zero_h[:, :], 0.0).then_inc(s_const, 1)
            e.memset(g.ones_h[:, :], 1.0).then_inc(s_const, 1)
            e.memset(g.ones_b[:, :], 1.0).then_inc(s_const, 1)
            e.wait_ge(s_sel, 3)
            e.wait_ge(s_bias, 16)
            split_bias(g, Chain(e, s_parts), e)
            e.wait_ge(s_x, 16 * NT)
            norm.vector(e)
            e.wait_ge(s_iota, 3)
            e.tensor_copy(g.iota_h[:, :], g.iota_i[:, 0:KW]).then_inc(s_const, 1)
            e.tensor_copy(g.block0[:, :], g.iota_i[:, KW:KW + P]).then_inc(s_const, 1)
            e.tensor_copy(g.node[:, :], g.iota_i[:, KW + P:KW + P + NT]).then_inc(s_const, 1)
            e.tensor_copy(g.ident_h[:, :], g.ident[:, :]).then_inc(s_const, 1)
            e.tensor_scalar(g.ident_c[:, :], g.ident[:, :], COUNT, None, ALU.mult).then_inc(s_const, 1)
            step = Chain(e, s_chain)
            e.wait_ge(s_ld, 16 * len(loads))
            step(e.tensor_tensor(g.keep_sum[:, :], dst, before, ALU.is_equal))
            step(e.tensor_reduce(g.whole[:, :], g.keep_sum[:, :], AX.X, ALU.min))
            step(e.tensor_scalar(g.diag[:, 0, :], g.ident[:, :], g.whole[:, 0:1], None, ALU.mult))
            step(e.tensor_copy(dstf, dst_p))
            step(e.tensor_scalar(keyf, src_p, float(R), None, ALU.mult))
            step(e.tensor_tensor(keyf, keyf, rel_p, ALU.add))
            step(e.tensor_copy(g.firsts[:, :], dstf[:, ::P]))
            step(e.memset(g.keep_sum[:, 0:1], 0.0))
            step(e.tensor_scalar(g.keep_max[:, :], g.keep_sum[:, :], BIG, -BIG, ALU.mult, ALU.add))
            step(e.tensor_scalar(relf, g.key_src[:, 0:STEPS], float(R), None, ALU.mult))
            step(e.tensor_tensor(g.key_rel[:, 0:STEPS], relf, rel, ALU.add))
            assert step.n == all_steps

        @block.tensor
        def _(e):
            e.wait_ge(s_chain, 3)
            e.matmul(g.ps_t[:, 0, 0:P], g.ones[:, :], g.diag[:, 0, :], start=True, stop=True).then_inc(s_mat, 1)

    s_c = g.sem("chains")
    with nc.Block() as block:
        @block.vector
        def _(e):
            step = Chain(e, s_c)
            step(e.tensor_copy(g.chain_sum[:, :], g.ps_t[:, 0, 0:P]))
            step(e.tensor_scalar(g.chain_max[:, :], g.chain_sum[:, :], BIG, -BIG, ALU.mult, ALU.add))


def locate_nodes(g, side):
    nc = g.nc
    s_c, s_p, s_rows = (g.sem(n) for n in ("lchain", "lprod", "lrows"))
    s_g = [g.sem(f"lgather{r}") for r in range(TROUNDS)]
    rounds = [slice(r * TILES, (r + 1) * TILES) for r in range(TROUNDS)]
    ready = [3 + (r + 1) * (TILES + 2) for r in range(TROUNDS)]
    firsts, junk = g.Z2[:, 0:BLOCKS], g.Z2[:, BLOCKS:2 * BLOCKS]
    half = BLOCKS // 2
    near = g.C[:, :, :]
    cmp = g.flat(g.msg)[:, 0:NT * P]
    cmp3 = cmp.rearrange("p (j c) -> p j c", j=NT)
    ends, begin, cnt, blk, t1, t2 = (g.small[:, c, :] for c in range(6))
    with nc.Block() as block:
        @block.vector
        def _(e):
            step = Chain(e, s_c)
            step(e.tensor_tensor(g.diag[:, :, :], g.ident[:, :].unsqueeze(1).to_broadcast([P, 7, P]),
                                 g.firsts[:, :].unsqueeze(2).to_broadcast([P, 7, P]), ALU.mult))
            e.wait_ge(s_p, 1)
            step(e.tensor_copy(firsts[:, 0:half], g.ps_t[:, 1, 0:half]))
            e.wait_ge(s_p, 2)
            step(e.tensor_copy(firsts[:, half:], g.ps_t[:, 1, 0:half]))
            for r, at in enumerate(rounds):
                for j in range(at.start, at.stop):
                    step(e.tensor_scalar(junk, firsts, g.node[:, j:j + 1], 0.0, ALU.is_le, ALU.add,
                                         accum_out=cnt[:, j:j + 1]))
                step(e.tensor_scalar(blk[:, at], cnt[:, at], -1.0, 0.0, ALU.add, ALU.max))
                step(e.tensor_copy(g.near_at[:, at], blk[:, at]))
                assert step.n == ready[r]
            for r, at in enumerate(rounds):
                e.wait_ge(s_g[r], 16 * TILES)
                step(e.tensor_tensor(cmp3[:, at, :], near[:, at, :],
                                     g.node[:, at].unsqueeze(2).to_broadcast([P, TILES, P]), ALU.is_le))
                step(e.tensor_reduce(cnt[:, at], cmp3[:, at, :], AX.X, ALU.add))
            step(e.tensor_scalar(blk, blk, float(P), None, ALU.mult))
            step(e.tensor_tensor(ends, blk, cnt, ALU.add))
            step(e.memset(g.ends1[:, 0:1], 0.0))
            step(e.tensor_copy(g.ends1[:, 1:NT + 1], ends))
            e.wait_ge(s_p, 3)
            step(e.tensor_copy(begin, g.ps_t[:, 1, 0:NT]))
            step(e.tensor_tensor(g.degree[:, :], ends, begin, ALU.subtract))
            step(e.tensor_scalar(t1, g.degree[:, :], 0.0, None, ALU.is_gt))
            step(e.tensor_scalar(ends, ends, -1.0, None, ALU.add))
            step(e.tensor_tensor(cmp3, ends.unsqueeze(2).to_broadcast([P, NT, P]),
                                 g.block0[:, :].unsqueeze(1).to_broadcast([P, NT, P]), ALU.is_ge))
            step(e.tensor_reduce(blk, cmp3, AX.X, ALU.add))
            step(e.tensor_scalar(blk, blk, -1.0, None, ALU.add))
            step(e.tensor_scalar(t2, blk, float(STEPS), None, ALU.mult))
            step(e.tensor_tensor(t2, begin, t2, ALU.is_lt))
            step(e.tensor_tensor(blk, blk, t2, ALU.mult))
            step(e.tensor_tensor(g.carry_at[:, :], blk, t1, ALU.mult))
            step(e.tensor_scalar(ends, ends, float(-P * STEPS), None, ALU.add))
            step(e.tensor_tensor(ends, ends, t1, ALU.mult))
            step(e.tensor_scalar(g.last_at[:, :], ends, float(P * STEPS), None, ALU.add))

        @block.tensor
        def _(e):
            e.wait_ge(s_c, 1)
            flat = g.diag[:, :, :].rearrange("p a b -> p (a b)")
            e.matmul(g.ps_t[:, 1, 0:half], g.ones[:, :], flat[:, 0:half], start=True, stop=True).then_inc(s_p, 1)
            e.wait_ge(s_c, 2)
            e.matmul(g.ps_t[:, 1, 0:half], g.ones[:, :], flat[:, half:], start=True, stop=True).then_inc(s_p, 1)
            side.tensor(e)
            e.wait_ge(s_c, ready[-1] + 2 * TROUNDS + 4)
            e.matmul(g.ps_t[:, 1, 0:NT], g.shift[:, :], g.ends1[:, 1:NT + 1], start=True, stop=False)
            e.matmul(g.ps_t[:, 1, 0:NT], g.corner[:, :], g.ends1[:, 0:NT], start=False, stop=True).then_inc(s_p, 1)

        @block.gpsimd
        def _(e):
            blocks = g.edge_list[0].rearrange("(b c) -> b c", c=P)
            for j in range(NT):
                if j % TILES == 0:
                    e.wait_ge(s_c, ready[j // TILES])
                e.indirect_dma_start(g.C[:, j, :], None, blocks,
                                     bass.IndirectOffsetOnAxis(g.near_at[:, j:j + 1], 0)).then_inc(s_g[j // TILES], 16)

        @block.scalar
        def _(e):
            for k in range(2):
                flat = g.edge_list[k]
                e.dma_start(g.edge_rows[:, k * P:(k + 1) * P],
                            bass.AP(flat.tensor, 0, [[SHIFT, STARTS], [1, P]])).then_inc(s_rows, 16)
            side.scalar(e)

        @block.sync
        def _(e):
            side.sync(e)
            e.wait_ge(s_rows, 32)


def locate_windows(g, side):
    nc = g.nc
    s_c, s_p, s_g, s_d, s_v, s_io, s_go = (g.sem(n) for n in (
        "wchain", "wprod", "wgather", "wdma", "wvec", "wiota", "wgo"))
    begin = g.small[:, 1, :]
    run = g.flat(g.run)
    dst, key = g.flat(g.msg)[:, 0:NW], g.flat(g.msg, I32)[:, NW:2 * NW]
    dst3, key3 = (x.rearrange("p (w g) -> p w g", g=GROUPS) for x in (dst, key))
    free = 2 * R * D
    ti, tk, tf, tg = g.CSI[:, 0:NW], g.arena[:, free:free + NW].bitcast(I32), g.arena[:, free + NW:free + 2 * NW], g.Z2[:, 0:NW]
    iota = g.hot.bitcast(I32)[:, 0:NW]
    low, spot = g.low, g.spot
    with nc.Block() as block:
        @block.tensor
        def _(e):
            e.transpose(g.ps_t[0:NT, 1, 0:P], begin, g.ident[:, :]).then_inc(s_p, 1)
            e.wait_ge(s_c, 2)
            side.tensor(e)
            e.wait_ge(s_g, 16 * GROUPS)
            for gr in range(GROUPS):
                if gr:
                    e.wait_ge(s_v, 2 * gr)
                for x in range(2):
                    at = gr * 2 * P + x * P
                    last = e.transpose(g.ps_t[:, 1, x * P:(x + 1) * P], run[:, at:at + P], g.ident[:, :])
                last.then_inc(s_p, 1)

        @block.vector
        def _(e):
            step = Chain(e, s_c)
            e.wait_ge(s_p, 1)
            step(e.tensor_copy(g.wrow[0:NT, :], g.ps_t[0:NT, 1, 0:P:WIN]))
            step(e.tensor_scalar(g.wrow[0:NT, :], g.wrow[0:NT, :], SHIFT.bit_length() - 1, None, ALU.arith_shift_right))
            e.wait_ge(s_io, 1)
            for gr in range(GROUPS):
                e.wait_ge(s_p, gr + 2)
                e.tensor_copy(dst3[:, :, gr], g.ps_t[:, 1, 0:P]).then_inc(s_v, 1)
                e.tensor_copy(key3[:, :, gr], g.ps_t[:, 1, P:2 * P]).then_inc(s_v, 1)
            e.wait_ge(s_v, 2 * GROUPS)
            step(e.tensor_scalar(ti, key, R.bit_length() - 1, P - 1, ALU.arith_shift_right, ALU.bitwise_and))
            step(e.tensor_copy(low, ti))
            step(e.tensor_scalar(ti, key, (R * P).bit_length() - 1, None, ALU.arith_shift_right))
            step(e.tensor_scalar(tk, key, R - 1, None, ALU.bitwise_and))
            step(e.tensor_tensor(spot, dst, iota, ALU.subtract))
            step(e.tensor_scalar(tf, spot, 0.0, float(WIN - 1), ALU.max, ALU.min))
            step(e.tensor_tensor(tg, tf, spot, ALU.is_equal))
            step(e.scalar_tensor_tensor(spot, ti, float(R * WIN), spot, ALU.mult, ALU.add))
            step(e.scalar_tensor_tensor(spot, tk, float(WIN), spot, ALU.mult, ALU.add))
            step(e.scalar_tensor_tensor(spot, spot, 1.0, tg, ALU.add, ALU.mult))
            step(e.tensor_scalar(spot, spot, -1.0, None, ALU.add))

        @block.sync
        def _(e):
            flat = g.window_rows.rearrange("(j u) -> j u", u=P // WIN)
            e.dma_start(flat[NT:NW * WIN // P, :], g.past[0:NW * WIN // P - NT, 0:P // WIN]).then_inc(s_d, 16)
            e.wait_ge(s_c, 2)
            e.dma_start(flat[0:NT, :], g.wrow[0:NT, :]).then_inc(s_d, 16)
            e.wait_ge(s_d, 32)
            e.dma_start(g.win_row[:, :], g.window_rows.rearrange("(p g) -> p g", g=GROUPS)).then_inc(s_d, 16)
            side.sync(e)

        block.scalar(side.scalar)

        @block.gpsimd
        def _(e):
            e.iota(iota, pattern=[[WIN, NW]], base=0, channel_multiplier=0).then_inc(s_io, 1)
            e.wait_ge(s_d, 48)
            e.sem_inc(s_go, 1)
            for gr in range(GROUPS):
                e.indirect_dma_start(run[:, gr * 2 * P:(gr + 1) * 2 * P], None, g.edge_rows,
                                     bass.IndirectOffsetOnAxis(g.win_row[:, gr:gr + 1], 0)).then_inc(s_g, 16)


class Norm:

    def __init__(self, g, src, gain=None, shift=None, relu=True):
        self.g, self.src, self.gain, self.shift, self.relu = g, src, gain, shift, relu
        self.s_chain, self.s_v, self.s_r, self.s_mean, self.s_sq, self.s_inv, self.s_own = (
            g.sem(n) for n in ("nchain", "var", "dev", "nmean", "nsquare", "ninv", "nown"))
    OURS = 2
    LAST = 10

    def vector(self, e):
        g, src = self.g, self.src
        step = Chain(e, self.s_chain)
        theirs = TROUNDS - self.OURS
        for r in range(theirs):
            at = slice(r * TILES, (r + 1) * TILES)
            step(e.tensor_reduce(g.mean[:, at], src[:, at, :], AX.X, ALU.add))
            e.tensor_scalar(g.mean[:, at], g.mean[:, at], -1.0 / D, None, ALU.mult).then_inc(self.s_mean, 1)
        at = slice(theirs * TILES, NT)
        wide = [P, self.OURS * TILES, D]
        step(e.tensor_reduce(g.mean[:, at], src[:, at, :], AX.X, ALU.add))
        step(e.tensor_scalar(g.mean[:, at], g.mean[:, at], -1.0 / D, None, ALU.mult))
        step(e.tensor_tensor(g.H[:, at, :], src[:, at, :], g.mean[:, at].unsqueeze(2).to_broadcast(wide), ALU.add))
        step(e.tensor_tensor(g.Z[:, at, :], g.H[:, at, :], g.H[:, at, :], ALU.mult))
        step(e.tensor_reduce(g.var[:, at], g.Z[:, at, :], AX.X, ALU.add))
        e.wait_ge(self.s_sq, 2 * theirs * TILES)
        e.tensor_scalar(g.var[:, :], g.var[:, :], 1.0 / D, 1e-5, ALU.mult, ALU.add).then_inc(self.s_v, 1)
        e.wait_ge(self.s_r, 1)
        e.reciprocal(g.inv_dev[:, :], g.dev[:, :]).then_inc(self.s_inv, 1)
        e.wait_ge(self.s_inv, 1)
        ours = slice(0, NT - self.LAST if self.relu else NT)
        n = ours.stop
        wide = [P, n, D]
        step(e.tensor_tensor(g.H[:, ours, :], g.H[:, ours, :], g.inv_dev[:, ours].unsqueeze(2).to_broadcast(wide), ALU.mult))
        if self.gain is not None:
            step(e.tensor_tensor(g.H[:, :, :], g.H[:, :, :], self.gain.unsqueeze(1).to_broadcast(wide), ALU.mult))
            step(e.tensor_tensor(g.H[:, :, :], g.H[:, :, :], self.shift.unsqueeze(1).to_broadcast(wide), ALU.add))
        if self.relu:
            step(e.tensor_scalar(g.H[:, ours, :], g.H[:, ours, :], 0.0, None, ALU.max))

    def scalar(self, e):
        g, theirs = self.g, TROUNDS - self.OURS
        for n in range(theirs * TILES):
            if n % TILES == 0:
                e.wait_ge(self.s_mean, n // TILES + 1)
            e.activation(g.H[:, n, :], self.src[:, n, :], ACT.Identity, bias=g.mean[:, n:n + 1]).then_inc(self.s_sq, 1)
            if n:
                self.square(e, n - 1)
        self.square(e, theirs * TILES - 1)
        e.wait_ge(self.s_v, 1)
        e.activation(g.dev[:, :], g.var[:, :], ACT.Sqrt).then_inc(self.s_r, 1)
        if self.relu:
            e.wait_ge(self.s_inv, 1)
            for n in range(NT - self.LAST, NT):
                e.activation(g.H[:, n, :], g.H[:, n, :], ACT.Relu, scale=g.inv_dev[:, n:n + 1]).then_inc(self.s_own, 1)

    def square(self, e, n):
        g = self.g
        e.wait_ge(self.s_sq, 2 * n + (2 if n < (TROUNDS - self.OURS) * TILES - 1 else 1))
        e.activation(g.Z[:, n, :], g.H[:, n, :], ACT.Square, accum_out=g.var[:, n:n + 1]).then_inc(self.s_sq, 1)


def layer_norm(g, gain=None, shift=None, relu=True, sync=None):
    norm = Norm(g, g.X if gain is None else g.Y, gain, shift, relu)
    with g.nc.Block() as block:
        block.vector(norm.vector)
        block.scalar(norm.scalar)
        if sync:
            block.sync(sync)


def back(k):
    return 1 if k == 0 else 2


class SideProjection:

    def __init__(self, g, first, count):
        self.g, self.first, self.count = g, first, count
        self.s_in, self.s_T, self.s_hT, self.s_mm, self.s_ev = (g.sem(n) for n in (
            "qin", "qtrans", "qcopy", "qprod", "qevac"))
        self.s_st = [g.sem(f"qstore{i}") for i in range(2)]

    def tiles(self, e, f):
        pairs = (self.count - 3) // 2
        with e.Fori(0, pairs) as i:
            for k in range(2):
                f(i * 2 + k, k, 3)
        for n in range(2 * pairs, self.count):
            f(n, n % 2, min(3, self.count - 1 - n))

    def tensor(self, e):
        g = self.g

        def transpose(n, slot):
            e.wait_ge(self.s_in, n + 1)
            e.wait_ge(self.s_hT, n + 2)
            e.transpose(g.ps_t[:, 0, 0:P], g.tin[:, slot, :], g.ident[:, :]).then_inc(self.s_T, 1)

        def tile(n, slot, follow):
            e.wait_ge(self.s_hT, n + 3)
            e.wait_ge(self.s_ev, n + 1)
            for a in range(0, W9, 512):
                b = min(a + 512, W9)
                e.matmul(g.ps_out[:, slot, a:b], g.tT[:, slot, :], g.w9[:, a:b], start=True, stop=False)
                last = e.matmul(g.ps_out[:, slot, a:b], g.ones_b[0:3, :], g.bias_parts[0:3, a:b], start=False, stop=True)
            last.then_inc(self.s_mm, 1)
            if follow >= 2:
                transpose(n + 2, slot)
        e.sem_inc(self.s_mm, 2)
        e.sem_inc(self.s_T, 2)
        transpose(0, 0)
        transpose(1, 1)
        self.tiles(e, tile)

    def scalar(self, e):
        g = self.g

        def copy_in(n, slot):
            e.wait_ge(self.s_T, n + 1)
            e.activation(g.tin[:, slot, :], g.H[:, self.tile(n), :].rearrange("p a f -> p (a f)"),
                         ACT.Copy).then_inc(self.s_in, 1)

        def copy_back(n, slot):
            e.wait_ge(self.s_T, n + 3)
            e.wait_ge(self.s_mm, n + 1)
            e.activation(g.tT[:, slot, :], g.ps_t[:, 0, 0:P], ACT.Copy).then_inc(self.s_hT, 1)

        def tile(n, slot, follow):
            if follow >= 2:
                copy_back(n + 2, slot)
            e.wait_ge(self.s_st[slot], self.half(n) * 16 + 16)
            e.wait_ge(self.s_mm, n + 3)
            e.activation(g.S[:, self.tile(n), :].rearrange("p a f -> p (a f)"), g.ps_out[:, slot, R * D:W9], ACT.Copy)
            e.activation(g.stage[:, slot, :], g.ps_out[:, slot, 0:R * D], ACT.Copy).then_inc(self.s_ev, 1)
            if follow >= 3:
                copy_in(n + 3, 1 - slot)
        e.sem_inc(self.s_hT, 2)
        e.sem_inc(self.s_ev, 2)
        for n in range(2):
            copy_in(n, n)
            copy_back(n, n)
        copy_in(2, 0)
        pairs = (self.count - 3) // 2
        with e.Fori(0, pairs) as i:
            self.half = lambda n: i
            for k in range(2):
                tile(i * 2 + k, k, 3)
        self.half = lambda n: n // 2
        for n in range(2 * pairs, self.count):
            tile(n, n % 2, min(3, self.count - 1 - n))

    def tile(self, n):
        return bass.ds(n + self.first, 1)

    def sync(self, e):
        g = self.g
        for s in range(2):
            e.dma_start(g.credit[s:s + 1, :], g.ident[0:1, 0:1]).then_inc(self.s_st[s], 16)

        def tile(n, slot, follow):
            e.wait_ge(self.s_ev, n + 3)
            e.dma_start(g.table8.rearrange("(m p r) f -> p m (r f)", p=P, r=R)[:, self.tile(n), :].rearrange(
                "p a f -> p (a f)"), g.stage[:, slot, :]).then_inc(self.s_st[slot], 16)
        self.tiles(e, tile)
        e.wait_ge(self.s_st[0], 16 * ((self.count + 1) // 2 + 1))
        e.wait_ge(self.s_st[1], 16 * (self.count // 2 + 1))


def project(g, src, weights, cols, evacuate, hidden=None, store=None):
    nc = g.nc
    s_in, s_T, s_hT, s_mm, s_ev, s_h1, s_h2 = (g.sem(n) for n in (
        "pin", "ptrans", "pcopy", "pprod", "pevac", "phid", "prelu"))
    s_st = [g.sem(f"pstore{i}") for i in range(2)]
    stages = [(c, min(c + 512, cols)) for c in range(0, cols, 512)]

    def body(e, f):
        with e.Fori(0, TROUNDS) as i:
            for k in range(TILES):
                f(i * TILES + k, k, k % 2)

    with nc.Block() as block:
        @block.scalar
        def _(e):
            def tile(n, k, s):
                e.wait_ge(s_T, n - back(k) + 3)
                e.activation(g.tin[:, s, :], src[:, bass.ds(n, 1), :].rearrange("p a f -> p (a f)"),
                             ACT.Copy).then_inc(s_in, 1)
                e.wait_ge(s_T, n + 3)
                e.wait_ge(s_mm, n - back(k) + 3)
                e.activation(g.tT[:, s, :], g.ps_t[:, s, 0:P], ACT.Copy).then_inc(s_hT, 1)
                if hidden:
                    e.wait_ge(s_h1, n + 1)
                    e.activation(g.tH[:, s, :], g.ps_t[:, s, P:2 * P], ACT.Relu, bias=hidden[1],
                                 scale=hidden[0]).then_inc(s_h2, 1)
            body(e, tile)

        @block.tensor
        def _(e):
            e.sem_inc(s_T, 2)
            e.sem_inc(s_mm, 2)

            def transpose(n, k, s):
                e.wait_ge(s_in, n + 1)
                e.wait_ge(s_hT, n - back(k) + 3)
                e.transpose(g.ps_t[:, s, 0:P], g.tin[:, s, :], g.ident[:, :]).then_inc(s_T, 1)

            def tile(n, k, s):
                if hidden or k == 0:
                    transpose(n, k, s)
                if not hidden and k + 1 < TILES:
                    transpose(n + 1, k + 1, 1 - s)
                e.wait_ge(s_hT, n + 3)
                if hidden:
                    e.matmul(g.ps_t[:, s, P:2 * P], weights, g.tT[:, s, :], start=True, stop=True).then_inc(s_h1, 1)
                    e.wait_ge(s_h2, n + 1)
                rows, w = (g.tH, hidden[2]) if hidden else (g.tT, weights)
                e.wait_ge(s_ev, n - back(k) + 3)
                for a, b in stages:
                    last = e.matmul(g.ps_out[:, s, a:b], rows[:, s, :], w[:, a:b], start=True, stop=True)
                last.then_inc(s_mm, 1)
            body(e, tile)

        @block.vector
        def _(e):
            e.sem_inc(s_hT, 2)
            e.sem_inc(s_ev, 2)

            def tile(n, k, s):
                e.wait_ge(s_mm, n + 3)
                if store:
                    per, done = (3, (k + 1) // 2) if s == 0 else (2, k // 2)
                    e.wait_ge(s_st[s], (i_of(n, k) * per + done) * 16 + 16)
                evacuate(e, n, s).then_inc(s_ev, 1)

            def i_of(n, k):
                return rounds[0]
            rounds = [None]
            with e.Fori(0, TROUNDS) as i:
                rounds[0] = i
                for k in range(TILES):
                    tile(i * TILES + k, k, k % 2)

        if store:
            @block.sync
            def _(e):
                for s in range(2):
                    e.dma_start(g.credit[s:s + 1, :], g.ident[0:1, 0:1]).then_inc(s_st[s], 16)

                def tile(n, k, s):
                    e.wait_ge(s_ev, n + 3)
                    store(e, n, s).then_inc(s_st[s], 16)
                body(e, tile)
                e.wait_ge(s_st[0], 16 * (3 * TROUNDS + 1))
                e.wait_ge(s_st[1], 16 * (2 * TROUNDS + 1))


def aggregate(g, table, key, op, build=False):
    nc = g.nc
    adds = op == ALU.add
    keep, chain = (g.keep_sum, g.chain_sum) if adds else (g.keep_max, g.chain_max)
    join = ALU.mult if adds else ALU.add
    s_msg = [g.sem(f"msg{q}") for q in range(NG)]
    s_out = [g.sem(f"rout{h}") for h in range(2)]
    s_idx, s_run, s_go = g.sem("idx"), g.sem("run"), g.sem("go")
    s_hot, s_cnt, s_adj, s_sum, s_plain, s_one, s_clr = (
        g.sem(n) for n in ("hot", "count", "adj", "sum", "plain", "plainstore", "clear"))
    s_sto = [g.sem(f"adjstore{h}") for h in range(2)]
    both = 2 * HALF
    ahead = both + 1
    npc = len(PIECES)
    running = g.running[0:P * STEPS, :].rearrange("(p t) f -> p t f", t=STEPS)

    def counts(k):
        return [g.ps_out[:, k % 2, q * 512:q * 512 + KW] for q in range(PAIR)]

    def plain(h, c):
        return g.adj1[:, PIECES[c][0]:PIECES[c][1], h * HD:(h + 1) * HD]

    def bank(c):
        return g.ps_t[:, c % 2, 0:(PIECES[c][1] - PIECES[c][0]) * HD]

    with nc.Block() as block:
        @block.gpsimd
        def _(e):
            def indices(q, t):
                e.tensor_copy(g.idx[:, q, :], key[:, bass.ds(t, GROUP)]).then_inc(s_idx, 1)

            indices(0, 0)
            with e.Fori(0, ROUNDS) as i:
                for q in range(NG):
                    e.wait_ge(s_idx, i * NG + (q + 1))
                    e.sem_inc(s_go, 1)
                    for k in range(GROUP):
                        if k == 1:
                            e.wait_ge(s_run, i * both + ((q + 2) * GROUP + 1))
                            e.sem_inc(s_go, 1)
                            indices((q + 1) % NG, i * both + (q + 1) * GROUP)
                        u = q * GROUP + k
                        e.indirect_dma_start(g.msg[:, u // HALF, u % HALF, :], None, table,
                                             bass.IndirectOffsetOnAxis(g.idx[:, q, k:k + 1], 0)).then_inc(s_msg[q], 16)

        @block.vector
        def _(e):
            e.memset(g.run[:, 1, HALF - 1, :], 0.0 if adds else -BIG).then_inc(s_run, 1)
            e.sem_inc(s_run, both)
            if build:
                e.memset(g.slot(1, R * NT * HD, F32), 0.0).then_inc(s_clr, 1)
                e.memset(g.one_u8, 0).then_inc(s_clr, 1)
            with e.Fori(0, ROUNDS) as i:
                for u in range(both):
                    h, k = u // HALF, u % HALF
                    if u % GROUP == 0:
                        e.wait_ge(s_msg[u // GROUP], i * (16 * GROUP) + 16 * GROUP)
                    if k == 0:
                        e.wait_ge(s_out[h], i * 16 + 16)
                    prev = g.run[:, h, k - 1, :] if k else g.run[:, 1 - h, HALF - 1, :]
                    t = i * both + u
                    e.wait_ge(s_run, t + ahead)
                    e.scalar_tensor_tensor(g.run[:, h, k, :], prev, keep[:, bass.ds(t, 1)], g.msg[:, h, k, :],
                                           join, op).then_inc(s_run, 1)
                    if not build:
                        continue
                    e.wait_ge(s_cnt, t + 1)
                    for q in range(PAIR):
                        w = bass.ds(t * PAIR + q, 1)
                        e.tensor_scalar(g.hot_low[:, u % RING, q, :], g.iota_h[:, 0:P], g.low[:, w],
                                        None, ALU.is_equal).then_inc(s_hot, 1)
                        e.tensor_scalar(g.hot_spot[:, u % RING, q, :], g.iota_h[:, :], g.spot[:, w],
                                        None, ALU.is_equal).then_inc(s_hot, 1)

        if build:
            def piece(e, h, c, n, steps):
                lo, hi = PIECES[c]
                e.wait_ge(s_plain, n + 1)
                e.sem_inc(s_go, 1)
                for r in steps:
                    last = e.matmul(bank(c), g.ident_h[:, :], g.half_f8(h)[:, lo:hi, r, :], start=r == 0, stop=r == R - 1)
                if R - 1 in steps:
                    last.then_inc(s_sum, 1)

            def total(e, h, c, n):
                e.wait_ge(s_plain, n + 3)
                e.sem_inc(s_go, 1)
                return e.matmul(g.ps_out[0:1, 0, 1024:1024 + (PIECES[c][1] - PIECES[c][0]) * HD], g.ones_h[:, 0:1],
                                plain(h, c), start=False, stop=False)

            def nothing(e, start=False, stop=False):
                e.matmul(g.ps_out[0:1, 0, 1024:1536], g.zero_h[:, 0:1], g.iota_h[:, 0:1].to_broadcast([P, 512]),
                         start=start, stop=stop)

            def copy_piece(e, h, c, n):
                e.wait_ge(s_sum, n + 2)
                e.sem_inc(s_go, 1)
                e.activation(plain(h, c), bank(c).rearrange("p (a n) -> p a n", n=HD), ACT.Copy,
                             saturate=True).then_inc(s_plain, 1)

            @block.tensor
            def _(e):
                e.sem_inc(s_cnt, RING)
                e.sem_inc(s_sum, 1)
                nothing(e, start=True)
                e.wait_ge(s_clr, 2)
                with e.Fori(0, ROUNDS) as i:
                    for u in range(both):
                        t = i * both + u
                        h = u // HALF
                        e.wait_ge(s_hot, (t + 1) * (2 * PAIR))
                        e.wait_ge(s_adj, t + 1)
                        for q in range(PAIR):
                            last = e.matmul(counts(u)[q], g.hot_low[:, u % RING, q, :], g.hot_spot[:, u % RING, q, :],
                                            start=True, stop=True)
                        last.then_inc(s_cnt, 1)
                        if u % HALF == 0:
                            e.wait_ge(s_adj, t + 2)
                        c = u % HALF // GROUP
                        n = i * (2 * npc) + (h * npc + c)
                        if u % GROUP < 3:
                            piece(e, 1 - h, c, n, ((0, 1, 2), (3, 4, 5), (6, 7))[u % GROUP])
                        else:
                            hb, cb = ((1 - h, c - 1) if c else (h, npc - 1))
                            e.wait_ge(s_plain, n + 2)
                            e.sem_inc(s_go, 1)
                            e.matmul(g.ps_out[0:1, 0, 1024:1024 + (PIECES[cb][1] - PIECES[cb][0]) * HD],
                                     g.ones_h[:, 0:1], plain(hb, cb), start=False, stop=False)
                n = ROUNDS * 2 * npc
                total(e, 0, npc - 1, n - 1)
                e.wait_ge(s_adj, STEPS + 2)
                for c in range(npc):
                    piece(e, 1, c, n + c, range(R))
                for c in range(npc):
                    total(e, 1, c, n + c)
                nothing(e, stop=True)

            @block.scalar
            def _(e):
                e.wait_ge(s_clr, 2)
                e.sem_inc(s_adj, 2)
                e.sem_inc(s_plain, 2)
                with e.Fori(0, ROUNDS) as i:
                    for u in range(both):
                        h, w = u // HALF, u % HALF * PAIR * WIN
                        if u % HALF == 0:
                            e.wait_ge(s_sto[h], i * 16 + 16)
                            e.wait_ge(s_sum, i * (2 * npc) + (h * npc + 1))
                            e.sem_inc(s_go, 1)
                        e.wait_ge(s_cnt, i * both + (u + RING + 1))
                        e.sem_inc(s_go, 1)
                        e.activation(g.half[h].rearrange("p (a n) -> p a n", n=HD)[:, :, w:w + PAIR * WIN].rearrange(
                            "p a (q n) -> p q a n", q=PAIR),
                            g.ps_out[:, u % 2, 0:1024].rearrange("p (q a) -> p q a", q=PAIR)[:, :, 0:KW].rearrange(
                                "p q (a n) -> p q a n", n=WIN), ACT.Copy, scale=COUNT, saturate=True).then_inc(s_adj, 1)
                        if u % GROUP == GROUP - 1:
                            c = u % HALF // GROUP
                            if u == HALF + GROUP - 1:
                                e.wait_ge(s_one, i * 16 + 16)
                                e.sem_inc(s_go, 1)
                            copy_piece(e, 1 - h, c, i * (2 * npc) + (h * npc + c))
                for c in range(npc):
                    copy_piece(e, 1, c, ROUNDS * 2 * npc + c)

        @block.sync
        def _(e):
            for h in range(2):
                e.dma_start(g.credit[h:h + 1, :], g.ident[0:1, 0:1]).then_inc(s_out[h], 16)
                if build:
                    e.dma_start(g.credit[2 + h:3 + h, :], g.ident[0:1, 0:1]).then_inc(s_sto[h], 16)

            def store_tile(at, n):
                e.wait_ge(s_plain, n + 2)
                e.sem_inc(s_go, 1)
                e.dma_start(g.adjacency1[at, :, :].rearrange("a p c -> (a p) c"), g.one_u8).then_inc(s_one, 16)

            with e.Fori(0, ROUNDS) as i:
                for h in range(2):
                    if build and h == 0:
                        store_tile(bass.ds(i, 1), i * (2 * npc) + npc)
                    e.wait_ge(s_run, i * both + (h + 1) * HALF + ahead)
                    e.dma_start(running[:, bass.ds(i * both + h * HALF, HALF), :],
                                g.run[:, h, :, :]).then_inc(s_out[h], 16)
                    if build:
                        e.wait_ge(s_adj, i * both + ((h + 1) * HALF + 2))
                        e.sem_inc(s_go, 1)
                        e.dma_start(g.adjacency[bass.ds(i * 2 + h, 1), :, :].rearrange("a p c -> (a p) c"),
                                    g.half_u8(h)).then_inc(s_sto[h], 16)
            for h in range(2):
                e.wait_ge(s_out[h], 16 * (ROUNDS + 1))
            if build:
                store_tile(slice(ROUNDS, ROUNDS + 1), ROUNDS * 2 * npc + npc)
                for h in range(2):
                    e.wait_ge(s_sto[h], 16 * (ROUNDS + 1))
                e.wait_ge(s_one, 16 * (ROUNDS + 1))

    s_t, s_s, s_c, s_a, s_b, s_hot, s_up, s_copy, s_pick, s_put = (g.sem(n) for n in (
        "ctrans", "cscan", "ccopy", "agather", "cchain", "chot", "chottrans", "chotcopy", "cpick", "cput"))
    hot = g.arena[:, 0:NT * P].rearrange("p (j c) -> p j c", j=NT)
    none = g.mean
    with nc.Block() as block:
        @block.gpsimd
        def _(e):
            for j in range(NT):
                e.indirect_dma_start(g.Z[:, j, :], None, g.running,
                                     bass.IndirectOffsetOnAxis(g.last_at[:, j:j + 1], 0)).then_inc(s_a, 16)

        @block.tensor
        def _(e):
            def transpose(j):
                e.wait_ge(s_hot, 1)
                if j >= 2:
                    e.wait_ge(s_copy, j - 1)
                e.transpose(g.ps_out[:, 1, (j % 2) * 512:(j % 2) * 512 + P], hot[:, j, :], g.ident[:, :]).then_inc(s_up, 1)
            e.transpose(g.ps_t[:, 0, 0:P], g.run[:, 1, HALF - 1, :], g.ident[:, :]).then_inc(s_t, 1)
            transpose(0)
            transpose(1)
            e.wait_ge(s_s, 1)
            e.transpose(g.ps_t[:, 1, 0:P], g.tT[:, 0, :], g.ident[:, :]).then_inc(s_t, 1)
            e.wait_ge(s_c, 1)
            for j in range(NT):
                e.wait_ge(s_copy, j + 1)
                if j >= 2:
                    e.wait_ge(s_put, j - 1)
                e.matmul(g.ps_out[:, 0, (j % 2) * 512:(j % 2) * 512 + D], g.tH[:, j % 2, :], g.tT[:, 1, :],
                         start=True, stop=True).then_inc(s_pick, 1)
                if j + 2 < NT:
                    transpose(j + 2)

        @block.scalar
        def _(e):
            for j in range(NT):
                e.wait_ge(s_up, j + 1)
                if j >= 2:
                    e.wait_ge(s_pick, j - 1)
                e.activation(g.tH[:, j % 2, :], g.ps_out[:, 1, (j % 2) * 512:(j % 2) * 512 + P],
                             ACT.Copy).then_inc(s_copy, 1)

        @block.vector
        def _(e):
            step = Chain(e, s_b)
            e.wait_ge(s_t, 1)
            e.tensor_tensor_scan(g.tT[:, 0, :], chain[:, :], g.ps_t[:, 0, 0:P], 0.0 if adds else -BIG,
                                 join, op).then_inc(s_s, 1)
            e.tensor_tensor(hot, g.iota_h[:, 1:P + 1].unsqueeze(1).to_broadcast([P, NT, P]),
                            g.carry_at[:, :].unsqueeze(2).to_broadcast([P, NT, P]), ALU.is_equal).then_inc(s_hot, 1)
            if adds:
                step(e.memset(none[:, :], 0.0))
            else:
                step(e.tensor_scalar(none[:, :], g.carry_at[:, :], 0.0, None, ALU.is_gt))
                step(e.tensor_scalar(none[:, :], none[:, :], BIG, -BIG, ALU.mult, ALU.add))
            e.wait_ge(s_t, 2)
            e.tensor_copy(g.tT[:, 1, :], g.ps_t[:, 1, 0:P]).then_inc(s_c, 1)
            for j in range(NT):
                e.wait_ge(s_pick, j + 1)
                e.tensor_scalar(g.C[:, j, :], g.ps_out[:, 0, (j % 2) * 512:(j % 2) * 512 + D], none[:, j:j + 1], None,
                                ALU.add).then_inc(s_put, 1)
            e.wait_ge(s_put, NT)
            e.wait_ge(s_a, 16 * NT)
            e.tensor_tensor(g.Z[:, :, :], g.Z[:, :, :], g.C[:, :, :], op)


def check_adjacency(g):
    nc = g.nc
    s_c = g.sem("kchain")
    with nc.Block() as block:
        @block.vector
        def _(e):
            step = Chain(e, s_c)
            step(e.tensor_reduce(g.check[:, :], g.ps_out[0:1, 0, 1024:1024 + PIECES[0][1] * HD], AX.X, ALU.add))
            step(e.tensor_scalar(g.flag[:, :], g.check[:, :], ALL, None, ALU.not_equal))


def early(g, params, relational=False):
    s = g.sem("early")
    if relational:
        parts = [load_half(g, m, m) for m in range(EARLY_HALVES)]
    else:
        parts = [(g.slot(k, NT * P, U8), g.adjacency1[k + 1]) for k in range(EARLY_ROUNDS * TILES)]

    parts = params + parts

    def stream(e):
        for part in parts:
            e.dma_start(*part).then_inc(s, 16)
        e.wait_ge(s, 16 * len(parts))
    return stream


def load_half(g, slot, m):
    at = slice(m, m + 1) if isinstance(m, int) else bass.ds(m, 1)
    return g.slot(slot, R * NT * HD, U8), g.adjacency[at, :, :].rearrange("a p c -> (a p) c")


def load_adjacency(g, e, s_ld):
    for k in range(EARLY_ROUNDS * TILES, NT):
        e.dma_start(g.slot(k, NT * P, U8), g.adjacency1[k + 1]).then_inc(s_ld[k // TILES], 16)


def cut_rows(g, e, scale, sem):
    for r in range(TROUNDS):
        at = slice(r * TILES, (r + 1) * TILES)
        e.tensor_scalar(g.cut[:, at, 0, :], g.H[:, at, :], scale, None, ALU.mult).then_inc(sem, 1)
        e.wait_ge(sem, 2 * r + 1)
        e.scalar_tensor_tensor(g.cut[:, at, 1, :], g.H[:, at, :], scale, g.cut[:, at, 0, :],
                               ALU.mult, ALU.subtract).then_inc(sem, 1)


class Sums:

    def __init__(self, g, hidden=None):
        self.g, self.hidden = g, hidden
        self.s_cut, self.s_ready, self.s_sum, self.s_z, self.s_prod, self.s_read, self.s_h1, self.s_h2, self.s_go = (
            g.sem(n) for n in ("mcut", "mready", "msum", "mz", "mprod", "mread", "mhid", "mrelu", "mgo"))
        self.z = g.SF[:, 0:2 * TILES * D].rearrange("p (s c) -> p s c", s=2)
        self.h = g.SF[:, 3 * TILES * D:4 * TILES * D]
        self.parts = ((0, 3), (3, TILES))

    def sums(self, i, q):
        lo, hi = self.parts[q]
        return self.g.ps_out[:, i % 2, q * 512:q * 512 + (hi - lo) * P]

    def out(self, q):
        lo, hi = self.parts[q]
        return self.g.ps_t[:, q, 0:(hi - lo) * P]

    def middle(self, q):
        lo, hi = self.parts[q]
        return self.g.ps_out[:, q, 1024:1024 + (hi - lo) * P]

    def tensor(self, e, i, cut, weights, base=0, parts_of=None):
        g, n = self.g, base * (2 * TROUNDS)

        def sums(q, tiles):
            lo, hi = self.parts[q]
            for a in tiles:
                adj = g.arena[:, i * TILES * NT * P // 4:(i + 1) * TILES * NT * P // 4].bitcast(F8).rearrange(
                    "p (k a n) -> p k a n", k=TILES, a=NT)[:, lo:hi, a, :]
                for part in range(2):
                    e.matmul(self.sums(i, q), cut[:, a, part, :], adj, start=a + part == 0, stop=False)
        if i == 0:
            for r in range(TROUNDS - 1):
                parts_of(r)
                sums(0, range(r * TILES, (r + 1) * TILES))
            sums(1, range(NT - TILES))
            parts_of(TROUNDS - 1)
        for q, (lo, hi) in enumerate(self.parts):
            if i >= 2:
                e.wait_ge(self.s_z, n + (2 * i - 2))
                e.sem_inc(self.s_go, 1)
            sums(q, range(NT) if i else range(NT - TILES, NT))
            for k in range(lo, hi):
                for part in range(2):
                    last = e.matmul(self.sums(i, q)[:, (k - lo) * P:(k - lo + 1) * P], cut[:, i * TILES + k, part, :],
                                    g.ident_c[:, :], start=False, stop=k == hi - 1 and part == 1)
            last.then_inc(self.s_sum, 1)
        for q, (lo, hi) in enumerate(self.parts):
            if self.hidden:
                e.wait_ge(self.s_z, n + (2 * i + q + 1))
                e.matmul(self.middle(q), self.hidden[2], self.z[:, i % 2, lo * P:hi * P], start=True,
                         stop=True).then_inc(self.s_h1, 1)
        for q, (lo, hi) in enumerate(self.parts):
            rows = self.z[:, i % 2, :]
            if self.hidden:
                rows = self.h
                e.wait_ge(self.s_h2, 2 * i + q + 1)
            else:
                e.wait_ge(self.s_z, n + (2 * i + q + 1))
            if i:
                e.wait_ge(self.s_read, n + (2 * i - 1 + q))
            for k in range(lo, hi):
                last = e.matmul(self.out(q)[:, (k - lo) * D:(k - lo + 1) * D], rows[:, k * P:(k + 1) * P], weights,
                                start=k == lo, stop=k == hi - 1)
            last.then_inc(self.s_prod, 1)

    def scalar(self, e, i, inverse, base=0):
        n = base * (2 * TROUNDS)
        for q, (lo, hi) in enumerate(self.parts):
            if i >= 2:
                e.wait_ge(self.s_prod, n + (2 * i - 2))
            e.wait_ge(self.s_sum, n + (2 * i + q + 1))
            e.sem_inc(self.s_go, 1)
            e.activation(self.z[:, i % 2, lo * P:hi * P], self.sums(i, q), ACT.Copy, scale=inverse).then_inc(self.s_z, 1)
        if self.hidden:
            for q, (lo, hi) in enumerate(self.parts):
                if i:
                    e.wait_ge(self.s_prod, 2 * i - 1 + q)
                e.wait_ge(self.s_h1, 2 * i + q + 1)
                e.activation(self.h[:, lo * P:hi * P], self.middle(q), ACT.Relu, bias=self.hidden[1],
                             scale=self.hidden[0]).then_inc(self.s_h2, 1)


def isomorphism_layer(g):
    m = Sums(g, hidden=(g.cols[:, 5:6], g.cols[:, 7:8], g.w9[:, 0:D]))
    s_ld = [g.sem(f"mload{k}") for k in range(TROUNDS)]
    s_c = g.sem("mchain")
    scale = 1024.0
    with g.nc.Block() as block:
        @block.gpsimd
        def _(e):
            e.sem_inc(m.s_go, 1)

        @block.sync
        def _(e):
            load_adjacency(g, e, s_ld)

        @block.vector
        def _(e):
            cut_rows(g, e, scale, m.s_cut)
            step = Chain(e, s_c)
            for i in range(TROUNDS):
                for q, (lo, hi) in enumerate(m.parts):
                    at = slice(i * TILES + lo, i * TILES + hi)
                    e.wait_ge(m.s_prod, 2 * i + q + 1)
                    e.tensor_tensor(g.Y[:, at, :], m.out(q).rearrange("p (k f) -> p k f", f=D),
                                    g.rows[:, 0, :].unsqueeze(1).to_broadcast([P, hi - lo, D]),
                                    ALU.add).then_inc(m.s_read, 1)
                    e.wait_ge(m.s_read, 2 * i + q + 1)
                    step(e.scalar_tensor_tensor(g.X[:, at, :], g.Y[:, at, :], 0.0, g.X[:, at, :], ALU.max, ALU.add))

        @block.scalar
        def _(e):
            for i in range(TROUNDS):
                m.scalar(e, i, 1.0 / (scale * COUNT))

        @block.tensor
        def _(e):
            def parts_of(r):
                e.wait_ge(m.s_cut, 2 * (r + 1))
                e.sem_inc(m.s_go, 1)
            for i in range(TROUNDS):
                if i >= EARLY_ROUNDS:
                    e.wait_ge(s_ld[i], 16 * TILES)
                e.sem_inc(m.s_go, 1)
                m.tensor(e, i, g.cut, g.w9[:, D:2 * D], parts_of=parts_of)


def layer_scales(g):
    def f(e, step):
        gains, shifts = (g.bias9[:, c * 4 * D:(c + 1) * 4 * D].rearrange("p (i f) -> p i f", f=D) for c in range(2))
        step(e.tensor_reduce(g.bounds[:, 0, :], gains, AX.X, ALU.max, apply_absolute_value=True))
        step(e.tensor_reduce(g.bounds[:, 1, :], shifts, AX.X, ALU.max, apply_absolute_value=True))
        step(e.scalar_tensor_tensor(g.bounds[:, 0, :], g.bounds[:, 0, :], float(np.sqrt(D)), g.bounds[:, 1, :],
                                    ALU.mult, ALU.add))
        step(e.tensor_scalar(g.bounds[:, 0, :], g.bounds[:, 0, :], 1e-30, 1.0 / TOP, ALU.max, ALU.mult))
        step(e.reciprocal(g.scale[:, 1:5], g.bounds[:, 0, :]))
        step(e.tensor_scalar(g.inverse[:, 1:5], g.bounds[:, 0, :], 1.0 / COUNT, None, ALU.mult))
        step(e.tensor_copy(g.scale[:, 0:1], g.unit[:, 0:1]))
        step(e.tensor_copy(g.inverse[:, 0:1], g.unit[:, 1:2]))
        step(e.tensor_tensor(g.dsc[:, :, :], g.dis[:, :].unsqueeze(1).to_broadcast([P, 5, NT]),
                             g.scale[:, :].unsqueeze(2).to_broadcast([P, 5, NT]), ALU.mult))
    vector_stage(g, f)


def graph_layers(g):
    m = Sums(g)
    s_ld = [g.sem(f"gload{k}") for k in range(TROUNDS)]
    s_c, s_v, s_r = g.sem("gchain"), g.sem("gvar"), g.sem("gdev")
    cuts = (g.cut, g.Z[:, :, :].rearrange("p j f -> p (j f)").bitcast(F16).rearrange("p (j a f) -> p j a f", a=2, f=D))
    T = g.SF[:, 2 * TILES * D:3 * TILES * D].rearrange("p (k f) -> p k f", f=D)
    wide = [P, TILES, D]
    CHAIN = 12

    def tall(x):
        return x.unsqueeze(1).to_broadcast(wide)

    with g.nc.Block() as block:
        @block.gpsimd
        def _(e):
            e.sem_inc(m.s_go, 1)

        @block.sync
        def _(e):
            load_adjacency(g, e, s_ld)

        def two_layers(e, f):
            with e.Fori(0, 2) as pair:
                for x in range(2):
                    f(pair * 2 + x, x)

        @block.vector
        def _(e):
            def split(x, i, scale, wait):
                at = slice(i * TILES, (i + 1) * TILES)
                wait(e.tensor_tensor(T, g.H[:, at, :], scale[:, at].unsqueeze(2).to_broadcast(wide), ALU.mult))
                wait(e.tensor_copy(cuts[x][:, at, 0, :], T))
                e.tensor_tensor(cuts[x][:, at, 1, :], T, cuts[x][:, at, 0, :], ALU.subtract).then_inc(m.s_cut, 1)

            first = Chain(e, g.sem("gfirst"))
            for i in range(TROUNDS):
                split(0, i, g.dsc[:, 0, :], first)
                e.wait_ge(m.s_cut, i + 1)

            def layer(n, x):
                for i in range(TROUNDS):
                    done = [0]

                    def step(ins):
                        done[0] += 1
                        ins.then_inc(s_c, 1)
                        e.wait_ge(s_c, n * (TROUNDS * CHAIN) + (i * CHAIN + done[0]))
                    at = slice(i * TILES, (i + 1) * TILES)
                    y, h = g.Y[:, at, :], g.H[:, at, :]
                    mean, var, dev = (v[:, at] for v in (g.mean, g.var, g.dev))
                    rows = [r[:, bass.ds(n * D, D)] for r in (g.w9[:, 4 * D:8 * D], g.bias9[:, 0:4 * D], g.bias9[:, 4 * D:8 * D])]
                    for q, (lo, hi) in enumerate(m.parts):
                        e.wait_ge(m.s_prod, n * (2 * TROUNDS) + (2 * i + q + 1))
                        e.tensor_tensor(y[:, lo:hi, :], m.out(q).rearrange("p (k f) -> p k f", f=D),
                                        g.dis[:, i * TILES + lo:i * TILES + hi].unsqueeze(2).to_broadcast([P, hi - lo, D]),
                                        ALU.mult).then_inc(m.s_read, 1)
                    e.wait_ge(m.s_read, n * (2 * TROUNDS) + (2 * i + 2))
                    step(e.tensor_tensor(y, y, tall(rows[0]), ALU.add))
                    step(e.scalar_tensor_tensor(y, y, 0.0, h, ALU.max, ALU.add))
                    step(e.tensor_reduce(mean, y, AX.X, ALU.add))
                    step(e.tensor_scalar(mean, mean, -1.0 / D, None, ALU.mult))
                    step(e.tensor_tensor(y, y, mean.unsqueeze(2).to_broadcast(wide), ALU.add))
                    step(e.tensor_tensor(T, y, y, ALU.mult))
                    step(e.tensor_reduce(var, T, AX.X, ALU.add))
                    e.tensor_scalar(var, var, 1.0 / D, 1e-5, ALU.mult, ALU.add).then_inc(s_v, 1)
                    e.wait_ge(s_r, n * TROUNDS + (i + 1))
                    step(e.reciprocal(mean, dev))
                    step(e.tensor_tensor(h, y, mean.unsqueeze(2).to_broadcast(wide), ALU.mult))
                    step(e.tensor_tensor(h, h, tall(rows[1]), ALU.mult))
                    step(e.tensor_tensor(h, h, tall(rows[2]), ALU.add))
                    nxt = g.dsc[:, bass.ds(n + 1, 1), :].rearrange("p a j -> p (a j)")
                    at = slice(i * TILES, (i + 1) * TILES)
                    step(e.tensor_tensor(T, h, nxt[:, at].unsqueeze(2).to_broadcast(wide), ALU.mult))
                    e.tensor_copy(cuts[1 - x][:, at, 0, :], T).then_inc(m.s_ready, 1)
                    e.wait_ge(m.s_ready, n * TROUNDS + (i + 1))
                    e.tensor_tensor(cuts[1 - x][:, at, 1, :], T, cuts[1 - x][:, at, 0, :], ALU.subtract).then_inc(m.s_cut, 1)
                    e.wait_ge(m.s_cut, (n + 1) * TROUNDS + (i + 1))
                    assert done[0] == CHAIN
            two_layers(e, layer)

        @block.scalar
        def _(e):
            def layer(n, x):
                for i in range(TROUNDS):
                    at = slice(i * TILES, (i + 1) * TILES)
                    m.scalar(e, i, g.inverse[:, bass.ds(n, 1)], base=n)
                    e.wait_ge(s_v, n * TROUNDS + (i + 1))
                    e.activation(g.dev[:, at], g.var[:, at], ACT.Sqrt).then_inc(s_r, 1)
            two_layers(e, layer)

        @block.tensor
        def _(e):
            for i in range(EARLY_ROUNDS, TROUNDS):
                e.wait_ge(s_ld[i], 16 * TILES)
                e.sem_inc(m.s_go, 1)

            def layer(n, x):
                def parts_of(r):
                    e.wait_ge(m.s_cut, n * TROUNDS + (r + 1))
                    e.sem_inc(m.s_go, 1)
                for i in range(TROUNDS):
                    m.tensor(e, i, cuts[x], g.w9[:, bass.ds(n * D, D)], base=n, parts_of=parts_of)
            two_layers(e, layer)


def relational_multiply(g, out, scale):
    nc = g.nc
    s_c, s_go, s_mm, s_ev, s_in, s_T, s_hT, s_p, s_o = (g.sem(n) for n in (
        "rcut", "rgo", "rprod", "revac", "rin", "rtrans", "rcopy", "rsum", "rout"))
    s_ld = [g.sem(f"rload{k}") for k in range(TILES)]
    halves = 2 * TILES
    order = []
    for j in range(halves):
        order.append(("half", j))
        if j >= 2 and j % 2 == 0:
            order.append(("tile", j // 2 - 1))
    order.append(("tile", TILES - 1))
    rows = g.Y[:, :, :].rearrange("p j f -> p (j f)")[:, 0:2 * R * P].rearrange("p (s r n) -> p s r n", s=2, r=R)
    with nc.Block() as block:
        @block.gpsimd
        def _(e):
            e.sem_inc(s_go, 1)

        @block.sync
        def _(e):
            for slot in range(EARLY_HALVES):
                e.dma_start(g.credit[slot:slot + 1, :], g.ident[0:1, 0:1]).then_inc(s_ld[slot], 16)
            for m in range(EARLY_HALVES, TILES):
                e.dma_start(*load_half(g, m, m)).then_inc(s_ld[m], 16)

            def reload(m, slot):
                e.wait_ge(s_mm, m + 1)
                e.sem_inc(s_go, 1)
                e.dma_start(*load_half(g, slot, m + TILES)).then_inc(s_ld[slot], 16)
            with e.Fori(0, TROUNDS - 1) as i:
                for j in range(halves):
                    reload(i * halves + j, j % TILES)
            for j in range(halves - TILES):
                reload((TROUNDS - 1) * halves + j, j % TILES)

        @block.vector
        def _(e):
            e.sem_inc(s_ev, 2)
            e.sem_inc(s_o, 2)
            cut_rows(g, e, scale[0], s_c)
            with e.Fori(0, TROUNDS) as i:
                for kind, j in order:
                    if kind == "half":
                        k, h = j // 2, j % 2
                        e.wait_ge(s_mm, i * halves + (j + 1))
                        e.wait_ge(s_p, i * TILES + (k - back(k) + 3))
                        e.tensor_scalar(rows[:, k % 2, :, h * HD:(h + 1) * HD],
                                        g.ps_out[:, h, 0:512].rearrange("p (r n) -> p r n", r=R), scale[1], None,
                                        ALU.mult).then_inc(s_ev, 1)
                    else:
                        n = i * TILES + j
                        e.wait_ge(s_p, n + 3)
                        e.tensor_tensor(out[:, bass.ds(n, 1), :].rearrange("p a f -> p (a f)"),
                                        g.ps_out[:, j % 2, 512:512 + D], g.bias9[:, R * D:W9], ALU.add).then_inc(s_o, 1)

        @block.scalar
        def _(e):
            with e.Fori(0, TROUNDS) as i:
                for k in range(TILES):
                    n = i * TILES + k
                    e.wait_ge(s_T, n - back(k) + 3)
                    e.activation(g.tin[:, k % 2, :], g.H[:, bass.ds(n, 1), :].rearrange("p a f -> p (a f)"),
                                 ACT.Copy).then_inc(s_in, 1)
                    e.wait_ge(s_T, n + 3)
                    e.wait_ge(s_p, n - back(k) + 3)
                    e.activation(g.tT[:, k % 2, :], g.ps_t[:, k % 2, 0:P], ACT.Copy).then_inc(s_hT, 1)

        @block.tensor
        def _(e):
            e.sem_inc(s_p, 2)
            e.sem_inc(s_T, 2)
            with e.Fori(0, TROUNDS) as i:
                for kind, j in order:
                    if kind == "half":
                        k, h = j // 2, j % 2
                        if h == 0:
                            e.wait_ge(s_in, i * TILES + (k + 1))
                            e.transpose(g.ps_t[:, k % 2, 0:P], g.tin[:, k % 2, :], g.ident[:, :]).then_inc(s_T, 1)
                        e.wait_ge(s_ld[j % TILES], i * 32 + (j // TILES * 16 + 16))
                        e.wait_ge(s_ev, i * halves + (j + 1))
                        e.sem_inc(s_go, 1)
                        adj = g.slot(j % TILES, R * NT * HD, F8).rearrange("p (a n) -> p a n", a=NT)
                        for a in range(NT):
                            if j == 0 and a % TILES == 0:
                                e.wait_ge(s_c, 2 * (a // TILES + 1))
                                e.sem_inc(s_go, 1)
                            for part in range(2):
                                last = e.matmul(g.ps_out[:, h, 0:512], g.cut[:, a, part, :], adj[:, a, :],
                                                start=a + part == 0, stop=a + part == NT)
                        last.then_inc(s_mm, 1)
                    else:
                        n = i * TILES + j
                        e.wait_ge(s_ev, (n + 1) * 2 + 2)
                        e.wait_ge(s_hT, n + 1)
                        e.wait_ge(s_o, n - back(j) + 3)
                        for r in range(R + 1):
                            lhs = rows[:, j % 2, r, :] if r < R else g.tT[:, j % 2, :]
                            last = e.matmul(g.ps_out[:, j % 2, 512:512 + D], lhs, g.w9[:, r * D:(r + 1) * D],
                                            start=r == 0, stop=r == R)
                        last.then_inc(s_p, 1)


def find_scale(g, src, sync=None):
    nc = g.nc
    s_c, s_p = g.sem("uchain"), g.sem("uprod")
    with nc.Block() as block:
        if sync:
            block.sync(sync)

        @block.vector
        def _(e):
            step = Chain(e, s_c)
            step(e.tensor_reduce(g.unit[:, 2:3], src[:, :, :], AX.XY, ALU.max, apply_absolute_value=True))
            e.wait_ge(s_p, 1)
            step(e.tensor_reduce(g.unit[0:1, 3:4], g.ps_t[0:1, 0, 0:P], AX.X, ALU.max))
            step(e.tensor_scalar(g.unit[0:1, 4:5], g.unit[0:1, 3:4], 1e-30, 1.0 / TOP, ALU.max, ALU.mult))
            step(e.reciprocal(g.unit[0:1, 3:4], g.unit[0:1, 4:5]))
            e.wait_ge(s_p, 2)
            step(e.tensor_copy(g.unit[:, 0:1], g.ps_t[:, 1, 0:1]))
            step(e.tensor_scalar(g.unit[:, 1:2], g.ps_t[:, 1, 1:2], 1.0 / COUNT, None, ALU.mult))

        @block.tensor
        def _(e):
            e.wait_ge(s_c, 1)
            e.transpose(g.ps_t[0:1, 0, 0:P], g.unit[:, 2:3], g.ident[:, :]).then_inc(s_p, 1)
            e.wait_ge(s_c, 4)
            e.matmul(g.ps_t[:, 1, 0:2], g.ones[0:1, :], g.unit[0:1, 3:5], start=True, stop=True).then_inc(s_p, 1)


def row(ap):
    return ap.rearrange("(a n) -> a n", a=1).to_broadcast([P, ap.shape[0]])


def vector_stage(g, f):
    s = g.sem("vstage")
    with g.nc.Block() as block:
        @block.vector
        def _(e):
            f(e, Chain(e, s))


def relational(g, table):
    def evacuate(e, n, s):
        e.tensor_tensor(g.stage[:, s, 0:512], g.ps_out[:, s, 0:512], g.bias9[:, 0:512], ALU.add)
        e.tensor_tensor(g.S[:, bass.ds(n, 1), :].rearrange("p a f -> p (a f)"), g.ps_out[:, s, R * D:W9],
                        g.bias9[:, R * D:W9], ALU.add)
        return e.tensor_tensor(g.stage[:, s, 512:1024], g.ps_out[:, s, 512:1024], g.bias9[:, 512:1024], ALU.add)

    def store(e, n, s):
        return e.dma_start(table.rearrange("(m p r) f -> p m (r f)", p=P, r=R)[:, bass.ds(n, 1), :].rearrange(
            "p a f -> p (a f)"), g.stage[:, s, :])
    project(g, g.H, g.w9, W9, evacuate, store=store)


def store_rows(g, src):
    s = g.sem("rows")
    with g.nc.Block() as block:
        @block.sync
        def _(e):
            e.dma_start(g.table1.rearrange("(j p) f -> p j f", p=P), src[:, :, :]).then_inc(s, 16)
            e.wait_ge(s, 16)


def nothing_to_do(g):
    s = g.sem("pass")
    with g.nc.Block() as block:
        for engine in (block.gpsimd, block.sync, block.vector, block.scalar, block.tensor):
            engine(lambda e: e.sem_inc(s, 1))


def load_flag(g):
    return g.nc.values_load(g.flag[0:1, 0:1], min_val=0, max_val=1,
                            skip_runtime_bounds_check_because="it is the result of a comparison")


def convolve(g, out, scale):
    with g.nc.If(load_flag(g)):
        vector_stage(g, lambda e, step: step(e.memset(g.bias9[:, 0:R * D], 0.0)))
        relational(g, g.table8)
        aggregate(g, g.table8, g.key_rel, ALU.add)
        vector_stage(g, lambda e, step: step(e.tensor_tensor(out[:, :, :], g.Z[:, :, :], g.S[:, :, :], ALU.add)))
    with g.nc.Else():
        relational_multiply(g, out, scale)
    g.nc.end_all_ifs()


def gnn_kernel(nc, a, out):
    with ExitStack() as ctx:
        g = Program(nc, ctx)
        g.x, g.src, g.dst, g.rel = (a[n] for n in ("x", "src", "dst", "edge_type_8"))
        g.running = g.dram("running_rows", [P * STEPS + 1, D])
        g.table8 = g.dram("table_rel", [NP * R, D])
        g.table1 = g.dram("table_node", [NP, D])
        g.edge_list = [g.dram(n, [P * PER]) for n in ("edge_dst", "edge_key")]
        g.edge_rows = g.dram("edge_rows", [STARTS, 2 * P])
        g.window_rows = g.dram("window_rows", [NW], I32)
        g.adjacency = g.dram("adjacency", [2 * NT, P, NT * R * HD], U8)
        g.adjacency1 = g.dram("adjacency_plain", [NT + 1, P, NT * P], U8)
        g.credit = g.dram("credit", [4, 1])
        g.X, g.H, g.Z = (g.sb(n, [P, NT, D]) for n in "XHZ")
        cs = g.sb("CS", [P, 2, NT, D])
        g.C = g.Y = cs[:, 0]
        g.S = cs[:, 1]
        g.CS = cs[:, :, :, :].rearrange("p a j f -> p (a j f)")
        g.CSI = g.CS.bitcast(I32)
        g.Z2 = g.Z[:, :, :].rearrange("p j f -> p (j f)")
        g.inv_dev = g.sb("inv_dev", [P, NT])
        g.mean, g.var, g.dev, g.degree, g.dis = (g.sb(n, [P, NT]) for n in ("mean", "var", "dev", "degree", "dis"))
        g.carry_at, g.last_at = g.sb("carry_at", [P, NT]), g.sb("last_at", [P, NT], I32)
        g.ident, g.shift, g.corner, g.ones, g.block0 = (g.sb(n, [P, P]) for n in ("ident", "shift", "corner", "ones", "block0"))
        g.chain_sum, g.chain_max = (g.sb(n, [P, P]) for n in ("chain_sum", "chain_max"))
        g.iota_i, g.iota_h = g.sb("iota_i", [P, KW + P + NT], I32), g.sb("iota_h", [P, KW], F16)
        g.past, g.wrow = (g.sb(n, [P, P // WIN], I32) for n in ("past", "wrow"))
        g.win_row = g.sb("win_row", [P, GROUPS], I32)
        g.near_at, g.node = g.sb("near_at", [P, NT], I32), g.sb("node", [P, NT])
        g.small, g.ends1 = g.sb("small", [P, 6, NT]), g.sb("ends1", [P, NT + 1])
        g.whole, g.firsts, g.diag = g.sb("whole", [P, 1]), g.sb("firsts", [P, 7]), g.sb("diag", [P, 7, P])
        words = R * NT * HD // 4
        sizes = [words, words, 2 * HALF * D, 2 * HALF * D, NW, NW, RING * PAIR * P // 2, RING * PAIR * KW // 2]
        at = [sum(sizes[:n]) for n in range(len(sizes) + 1)]
        g.arena = g.sb("arena", [P, max(at[-1], TILES * words, NT * NT * P // 4)])
        part = [g.arena[:, at[n]:at[n + 1]] for n in range(len(sizes))]
        g.slot = lambda k, size, dt: g.arena[:, k * size // 4:(k + 1) * size // 4].bitcast(dt)
        g.half = [g.slot(h, R * NT * HD, F8) for h in range(2)]
        g.half_u8 = lambda h: g.slot(h, R * NT * HD, U8)
        g.half_f8 = lambda h: g.half[h].rearrange("p (a r n) -> p a r n", a=NT, r=R)
        g.msg, g.run = (x.rearrange("p (a b c) -> p a b c", a=2, b=HALF) for x in part[2:4])
        g.low, g.spot = part[4:6]
        g.hot = g.arena[:, at[6]:at[8]]
        g.stage = g.arena[:, 0:2 * R * D].rearrange("p (s c) -> p s c", s=2)
        g.adj1 = g.sb("adj1", [P, NT, P], F8)
        g.one = g.adj1[:, :, :].rearrange("p h n -> p (h n)")
        g.one_u8 = g.one.bitcast(U8)
        g.hot_low, g.hot_spot = (x.bitcast(F16).rearrange("p (a b c) -> p a b c", a=RING, b=PAIR) for x in part[6:8])
        g.zero_h, g.ones_h, g.ident_h, g.ident_c = (g.sb(n, [P, P], F16) for n in ("zero_h", "ones_h", "ident_h", "ident_c"))
        g.cut = g.sb("cut", [P, NT, 2, D], F16)
        g.dsc, g.scale, g.inverse = g.sb("dsc", [P, 5, NT]), g.sb("scale", [P, 5]), g.sb("inverse", [P, 5])
        g.bounds = g.sb("bounds", [P, 2, 4])
        g.SF = g.S.rearrange("p j f -> p (j f)")
        g.check, g.flag, g.unit = g.sb("check", [1, 1]), g.sb("flag", [1, 1], I32), g.sb("unit", [P, 5])
        g.key_src, g.key_rel = (g.sb(n, [P, STEPS + HALF], I32) for n in ("key_src", "key_rel"))
        g.keep_sum, g.keep_max = (g.sb(n, [P, STEPS]) for n in ("keep_sum", "keep_max"))
        g.idx = g.sb("idx", [P, NG, GROUP], I32)
        g.tin, g.tT, g.tH = (g.sb(n, [P, 2, D]) for n in ("tin", "tT", "tH"))
        g.w9, g.bias9 = g.sb("w9", [P, W9]), g.sb("bias9", [P, W9])
        g.ones_b, g.bias_parts = g.sb("ones_b", [P, P], BF16), g.sb("bias_parts", [P, W9], BF16)
        g.rows = g.sb("rows", [P, 4, D])
        g.cols = g.sb("cols", [P, 8])
        g.ps_t = ctx.enter_context(nc.psum_tensor("ps_t", [P, 2, 512], F32))
        g.ps_out = ctx.enter_context(nc.psum_tensor("ps_out", [P, 2, 1536], F32))

        prepare(g, [(g.bias9[:, :], row(a["L0_gnn_bias"].rearrange("r o -> (r o)"))),
                    (g.w9[:, :].rearrange("k (r o) -> k r o", o=D), a["L0_gnn_weight"].rearrange("r k o -> k r o"))])
        locate_nodes(g, SideProjection(g, 0, NT - BESIDE))
        locate_windows(g, SideProjection(g, NT - BESIDE, BESIDE))
        aggregate(g, g.table8, g.key_rel, ALU.max, build=True)
        check_adjacency(g)

        def finish0(e, step):
            step(e.tensor_tensor(g.Z[:, :, :], g.Z[:, :, :], g.S[:, :, :], ALU.add))
            step(e.scalar_tensor_tensor(g.X[:, :, :], g.Z[:, :, :], 0.0, g.X[:, :, :], ALU.max, ALU.add))
        vector_stage(g, finish0)

        g.recycle()

        params = ([(g.w9[:, 0:D], a["L1_gnn_W1"]), (g.w9[:, D:2 * D], a["L1_gnn_W2"]),
                        (g.rows[:, 0, :], row(a["L1_gnn_b2"]))] +
                       [(g.cols[:, c:c + 1], a[f"L1_gnn_{n}"].rearrange("(p a) -> p a", a=1))
                        for c, n in enumerate(("b1", "gamma", "beta", "mov_mean", "mov_var"))])
        layer_norm(g, sync=early(g, params))
        s_v, s_r, s_n = g.sem("bnv"), g.sem("bnr"), g.sem("bnc")
        with nc.Block() as block:
            @block.vector
            def _(e):
                step = Chain(e, s_n)
                e.tensor_scalar(g.cols[:, 4:5], g.cols[:, 4:5], 0.001, None, ALU.add).then_inc(s_v, 1)
                step(e.tensor_tensor(g.cols[:, 0:1], g.cols[:, 0:1], g.cols[:, 3:4], ALU.subtract))
                e.wait_ge(s_r, 1)
                step(e.reciprocal(g.cols[:, 5:6], g.cols[:, 6:7]))
                step(e.tensor_tensor(g.cols[:, 5:6], g.cols[:, 5:6], g.cols[:, 1:2], ALU.mult))
                step(e.tensor_tensor(g.cols[:, 7:8], g.cols[:, 0:1], g.cols[:, 5:6], ALU.mult))
                step(e.tensor_tensor(g.cols[:, 7:8], g.cols[:, 7:8], g.cols[:, 2:3], ALU.add))

            @block.scalar
            def _(e):
                e.wait_ge(s_v, 1)
                e.activation(g.cols[:, 6:7], g.cols[:, 4:5], ACT.Sqrt).then_inc(s_r, 1)

        def evacuate1(e, n, s):
            return e.tensor_tensor(g.S[:, bass.ds(n, 1), :].rearrange("p a f -> p (a f)"), g.ps_out[:, s, 0:D],
                                   g.rows[:, 0, :], ALU.add)

        with nc.If(load_flag(g)):
            store_rows(g, g.H)
            aggregate(g, g.table1, g.key_src, ALU.add)
            vector_stage(g, lambda e, step: step(e.tensor_tensor(g.Z[:, :, :], g.Z[:, :, :], g.H[:, :, :], ALU.add)))
            project(g, g.Z, g.w9[:, 0:D], D, evacuate1, hidden=(g.cols[:, 5:6], g.cols[:, 7:8], g.w9[:, D:2 * D]))
            vector_stage(g, lambda e, step: step(e.scalar_tensor_tensor(
                g.X[:, :, :], g.S[:, :, :], 0.0, g.X[:, :, :], ALU.max, ALU.add)))
        with nc.Else():
            isomorphism_layer(g)
        nc.end_all_ifs()

        g.recycle()

        for n, first in (("1", True), ("2", False)):
            params = ([(g.w9[:, 0:R * D].rearrange("k (r o) -> k r o", o=D), a[f"L2_gnn_W{n}"].rearrange("r k o -> k r o")),
                            (g.w9[:, R * D:W9], a[f"L2_gnn_loop_w{n}"]),
                            (g.bias9[:, R * D:W9], row(a[f"L2_gnn_b{n}"]))])
            if first:
                layer_norm(g, sync=early(g, params, relational=True))
            else:
                find_scale(g, g.H, sync=early(g, params, relational=True))
            convolve(g, g.H if first else g.Z,
                     (1024.0, 1.0 / (1024.0 * COUNT)) if first else (g.unit[:, 0:1], g.unit[:, 1:2]))

            def finish2(e, step):
                if first:
                    step(e.tensor_scalar(g.H[:, :, :], g.H[:, :, :], 0.0, None, ALU.max))
                else:
                    step(e.tensor_tensor(g.X[:, :, :], g.Z[:, :, :], g.X[:, :, :], ALU.add))
            vector_stage(g, finish2)
            g.recycle()

        params = ([(g.w9[:, 8 * D:W9], a["L3_gnn_W_in"]), (g.bias9[:, 8 * D:W9], row(a["L3_gnn_b_in"])),
                        (g.w9[:, 0:4 * D].rearrange("k (i o) -> k i o", o=D), a["L3_gnn_Wc"].rearrange("i k o -> k i o"))] +
                    [(out_row, row(a[f"L3_gnn_{n}"].rearrange("i o -> (i o)"))) for n, out_row in (
                        ("bc", g.w9[:, 4 * D:8 * D]), ("ln_g", g.bias9[:, 0:4 * D]), ("ln_b", g.bias9[:, 4 * D:8 * D]))])
        layer_norm(g, sync=early(g, params))
        s_v, s_r, s_n = g.sem("gv"), g.sem("gr"), g.sem("gc")
        with nc.Block() as block:
            @block.vector
            def _(e):
                e.tensor_scalar(g.var[:, :], g.degree[:, :], 1.0, None, ALU.add).then_inc(s_v, 1)
                e.wait_ge(s_r, 1)
                e.reciprocal(g.dis[:, :], g.dev[:, :]).then_inc(s_n, 1)

            @block.scalar
            def _(e):
                e.wait_ge(s_v, 1)
                e.activation(g.dev[:, :], g.var[:, :], ACT.Sqrt).then_inc(s_r, 1)

        def evacuate_in(e, n, s):
            return e.tensor_tensor(g.S[:, bass.ds(n, 1), :].rearrange("p a f -> p (a f)"), g.ps_out[:, s, 0:D],
                                   g.bias9[:, 8 * D:W9], ALU.add)
        project(g, g.H, g.w9[:, 8 * D:W9], D, evacuate_in)

        def to_h(e, step):
            step(e.tensor_copy(g.H[:, :, :], g.S[:, :, :]))
        vector_stage(g, to_h)
        find_scale(g, g.H)
        layer_scales(g)
        g.recycle()
        for i in range(4):
            with nc.If(load_flag(g)):
                gain, shift = (g.bias9[:, c * D:(c + 1) * D] for c in (i, 4 + i))

                def evacuate_t(e, n, s):
                    return e.tensor_scalar(g.S[:, bass.ds(n, 1), :].rearrange("p a f -> p (a f)"), g.ps_out[:, s, 0:D],
                                           g.dis[:, bass.ds(n, 1)], None, ALU.mult)

                def combine(e, step):
                    step(e.tensor_tensor(g.S[:, :, :], g.S[:, :, :],
                                         g.w9[:, (4 + i) * D:(5 + i) * D].unsqueeze(1).to_broadcast([P, NT, D]), ALU.add))
                    step(e.scalar_tensor_tensor(g.Y[:, :, :], g.S[:, :, :], 0.0, g.H[:, :, :], ALU.max, ALU.add))
                vector_stage(g, lambda e, step: step(e.tensor_tensor(
                    g.S[:, :, :], g.H[:, :, :], g.dis[:, :].unsqueeze(2).to_broadcast([P, NT, D]), ALU.mult)))
                store_rows(g, g.S)
                aggregate(g, g.table1, g.key_src, ALU.add)
                vector_stage(g, lambda e, step: step(e.tensor_tensor(g.Z[:, :, :], g.Z[:, :, :], g.S[:, :, :], ALU.add)))
                project(g, g.Z, g.w9[:, i * D:(i + 1) * D], D, evacuate_t)
                vector_stage(g, combine)
                layer_norm(g, gain, shift, relu=False)
            with nc.Else():
                if i == 0:
                    graph_layers(g)
                else:
                    nothing_to_do(g)
            nc.end_all_ifs()
            g.recycle()

        def finish3(e, step):
            step(e.tensor_tensor(g.X[:, :, :], g.X[:, :, :], g.H[:, :, :], ALU.add))
        vector_stage(g, finish3)
        s_o = g.sem("out")
        with nc.Block() as block:
            @block.sync
            def _(e):
                e.dma_start(out[0:N - LAST, :].rearrange("(j p) f -> p j f", p=P), g.X[:, 0:NT - 1, :]).then_inc(s_o, 16)
                e.dma_start(out[N - LAST:N, :], g.X[0:LAST, NT - 1, :]).then_inc(s_o, 16)
                e.wait_ge(s_o, 32)


def kernel(**inputs):
    import concourse.bacc as bacc
    from concourse.bass_utils import run_bass_kernel_spmd

    nc = bacc.Bacc("TRN2", target_bir_lowering=False, num_devices=1)
    arrays, aps = {}, {}
    for name, value in inputs.items():
        value = np.ascontiguousarray(value)
        arrays[f"in_{name}"] = value
        aps[name] = nc.dram_tensor(f"in_{name}", value.shape, mybir.dt.from_np(value.dtype), kind="ExternalInput").ap()
    out = nc.dram_tensor("out_x", (N, D), F32, kind="ExternalOutput").ap()
    gnn_kernel(nc, aps, out)
    return run_bass_kernel_spmd(nc, [arrays], core_ids=[0]).results[0]["out_x"]
```
